# Optimizing a Trainium2 kernel written in Bass

```python
import numpy as np
import jax
import jax.numpy as jnp

def _softmax(x, axis=-1):
    return jax.nn.softmax(x, axis=axis)
def _gelu(x):
    return jax.nn.gelu(x, approximate=True)
def _silu(x):
    return jax.nn.silu(x)
def _sigmoid(x):
    return jax.nn.sigmoid(x)
def _layernorm(x, axis=-1, eps=1e-5):
    m = jnp.mean(x, axis=axis, keepdims=True)
    v = jnp.var(x, axis=axis, keepdims=True)
    return (x - m) / jnp.sqrt(v + eps)
def _scatter_add(tgt, idx, src, axis=0):
    return tgt.at[idx].add(src)
def _segment_sum(src, seg, n):
    return jax.ops.segment_sum(src, seg, n)

kernel_name = 'mk_conv_seq_d2_conv_nchw512_66f062'

def setup_inputs(seed: int = 0):
    np.random.seed(seed)
    _w = jnp.asarray
    def _rec_inputs():
        import jax
        import jax.numpy as jnp
        _gk = jax.random.key(seed)
        x = -0.0002928 + 1 * jax.random.normal(jax.random.fold_in(_gk, 1), (8, 512, 32, 32), jnp.float32)
        return x
    x = _rec_inputs()
    def _L0_conv_setup():
        import math
        import jax, jax.numpy as jnp
        import numpy as np
        B, C, H, W = (8, 512, 32, 32)
        NUM_HEADS = 8
        NUM_GROUPS = min(C // 4, 32)
        EPS = 1e-06

        def _group_norm(x, w, b):
            bsz, c, t = x.shape
            g = NUM_GROUPS
            xg = x.reshape(bsz, g, c // g, t)
            mean = jnp.mean(xg, axis=(2, 3), keepdims=True)
            var = jnp.var(xg, axis=(2, 3), keepdims=True)
            xn = ((xg - mean) * jax.lax.rsqrt(var + EPS)).reshape(bsz, c, t)
            return xn * w[None, :, None] + b[None, :, None]
        key = jax.random.key(seed)
        ks = jax.random.split(key, 7)
        x = jax.random.normal(ks[0], (B, C, H, W), dtype=jnp.float32)
        gn_w = jax.random.normal(ks[1], (C,), dtype=jnp.float32) * 0.02 + 1.0
        gn_b = jax.random.normal(ks[2], (C,), dtype=jnp.float32) * 0.02
        qkv_w = jax.random.normal(ks[3], (3 * C, C), dtype=jnp.float32) / math.sqrt(C)
        qkv_b = jax.random.normal(ks[4], (3 * C,), dtype=jnp.float32) * 0.02
        proj_w = jax.random.normal(ks[5], (C, C), dtype=jnp.float32) / math.sqrt(C)
        proj_b = jax.random.normal(ks[6], (C,), dtype=jnp.float32) * 0.02
        return {'x': x, 'gn_w': gn_w, 'gn_b': gn_b, 'qkv_w': qkv_w, 'qkv_b': qkv_b, 'proj_w': proj_w, 'proj_b': proj_b}
    _L0_conv_all = _L0_conv_setup()
    _L0_conv_in = {k: v for k, v in _L0_conv_all.items() if k in ('gn_w', 'gn_b', 'qkv_w', 'qkv_b', 'proj_w', 'proj_b', )}
    del _L0_conv_all

    def _L1_conv_setup():
        import jax, jax.numpy as jnp
        import numpy as np
        N_HEADS = 8
        key = jax.random.key(seed)
        k1, k2, k3 = jax.random.split(key, 3)
        B, C, H, W = (16, 512, 32, 32)
        x = jax.random.normal(k1, (B, C, H, W), dtype=jnp.float32)
        w_qkv = jax.random.normal(k2, (C, 3 * C), dtype=jnp.float32) * C ** (-0.5)
        b_qkv = jnp.zeros((3 * C,), dtype=jnp.float32)
        w_proj = jax.random.normal(k3, (C, C), dtype=jnp.float32) * C ** (-0.5)
        b_proj = jnp.zeros((C,), dtype=jnp.float32)
        return {'x': x, 'w_qkv': w_qkv, 'b_qkv': b_qkv, 'w_proj': w_proj, 'b_proj': b_proj}
    _L1_conv_all = _L1_conv_setup()
    _L1_conv_in = {k: v for k, v in _L1_conv_all.items() if k in ('w_qkv', 'b_qkv', 'w_proj', 'b_proj', )}
    del _L1_conv_all

    return {
        "x": x,
        "L0_conv_gn_w": _L0_conv_in["gn_w"],
        "L0_conv_gn_b": _L0_conv_in["gn_b"],
        "L0_conv_qkv_w": _L0_conv_in["qkv_w"],
        "L0_conv_qkv_b": _L0_conv_in["qkv_b"],
        "L0_conv_proj_w": _L0_conv_in["proj_w"],
        "L0_conv_proj_b": _L0_conv_in["proj_b"],
        "L1_conv_w_qkv": _L1_conv_in["w_qkv"],
        "L1_conv_b_qkv": _L1_conv_in["b_qkv"],
        "L1_conv_w_proj": _L1_conv_in["w_proj"],
        "L1_conv_b_proj": _L1_conv_in["b_proj"],
    }

def reference(x, L0_conv_gn_w, L0_conv_gn_b, L0_conv_qkv_w, L0_conv_qkv_b, L0_conv_proj_w, L0_conv_proj_b, L1_conv_w_qkv, L1_conv_b_qkv, L1_conv_w_proj, L1_conv_b_proj):
    import jax
    import jax.numpy as jnp
    def _L0_conv_ref(x, gn_w, gn_b, qkv_w, qkv_b, proj_w, proj_b):
        import math
        import jax, jax.numpy as jnp
        import numpy as np
        B, C, H, W = (8, 512, 32, 32)
        NUM_HEADS = 8
        NUM_GROUPS = min(C // 4, 32)
        EPS = 1e-06

        def _group_norm(x, w, b):
            bsz, c, t = x.shape
            g = NUM_GROUPS
            xg = x.reshape(bsz, g, c // g, t)
            mean = jnp.mean(xg, axis=(2, 3), keepdims=True)
            var = jnp.var(xg, axis=(2, 3), keepdims=True)
            xn = ((xg - mean) * jax.lax.rsqrt(var + EPS)).reshape(bsz, c, t)
            return xn * w[None, :, None] + b[None, :, None]
        b, c = (x.shape[0], x.shape[1])
        spatial = x.shape[2:]
        x2 = x.reshape(b, c, -1)
        t = x2.shape[-1]
        xn = _group_norm(x2, gn_w, gn_b)
        qkv = jnp.einsum('oc,bct->bot', qkv_w, xn) + qkv_b[None, :, None]
        n_heads = NUM_HEADS
        ch = c // n_heads
        qkv = qkv.reshape(b * n_heads, 3 * ch, t)
        q, k, v = (qkv[:, :ch], qkv[:, ch:2 * ch], qkv[:, 2 * ch:])
        scale = 1.0 / math.sqrt(math.sqrt(ch))
        weight = jnp.einsum('bct,bcs->bts', q * scale, k * scale)
        weight = jax.nn.softmax(weight.astype(jnp.float32), axis=-1).astype(weight.dtype)
        a = jnp.einsum('bts,bcs->bct', weight, v)
        h = a.reshape(b, c, t)
        h = jnp.einsum('oc,bct->bot', proj_w, h) + proj_b[None, :, None]
        out = (x2 + h).reshape(b, c, *spatial) / np.sqrt(2.0)
        return out

    def _L1_conv_ref(x, w_qkv, b_qkv, w_proj, b_proj):
        import jax, jax.numpy as jnp
        import numpy as np
        N_HEADS = 8
        B, C, H, W = x.shape
        S = H * W
        d_k = C // N_HEADS
        scale = d_k ** (-0.5)
        xr = x.reshape(B, C, S).transpose(0, 2, 1)
        qkv = (xr @ w_qkv + b_qkv).reshape(B, S, N_HEADS, 3 * d_k)
        q, k, v = jnp.split(qkv, 3, axis=-1)
        attn = jnp.einsum('bihd,bjhd->bijh', q, k) * scale
        attn = jax.nn.softmax(attn, axis=2)
        out = jnp.einsum('bijh,bjhd->bihd', attn, v).reshape(B, S, N_HEADS * d_k)
        out = out @ w_proj + b_proj
        out = out.transpose(0, 2, 1).reshape(B, C, H, W)
        return out + x

    def _gn(v, G=32, eps=1e-5):
        B_, C_, H_, W_ = v.shape
        g = v.reshape(B_, G, C_ // G, H_, W_)
        m = jnp.mean(g, axis=(2, 3, 4), keepdims=True)
        s = jnp.var(g, axis=(2, 3, 4), keepdims=True)
        return ((g - m) / jnp.sqrt(s + eps)).reshape(v.shape)

    def _ln_c(v, eps=1e-6):
        m = jnp.mean(v, axis=1, keepdims=True)
        s = jnp.var(v, axis=1, keepdims=True)
        return (v - m) / jnp.sqrt(s + eps)

    def _ln_t(v, eps=1e-5):
        m = jnp.mean(v, axis=-1, keepdims=True)
        s = jnp.var(v, axis=-1, keepdims=True)
        return (v - m) / jnp.sqrt(s + eps)

    def _to_tokens(v):
        B_, C_, H_, W_ = v.shape
        return v.reshape(B_, C_, H_ * W_).transpose(0, 2, 1)
    def _from_tokens(t, like):
        B_, C_, H_, W_ = like.shape
        return t.transpose(0, 2, 1).reshape(B_, C_, H_, W_)

    x = _L0_conv_ref(x, L0_conv_gn_w, L0_conv_gn_b, L0_conv_qkv_w, L0_conv_qkv_b, L0_conv_proj_w, L0_conv_proj_b)
    x = _L1_conv_ref(x, L1_conv_w_qkv, L1_conv_b_qkv, L1_conv_w_proj, L1_conv_b_proj)
    return x


_drawn_inputs = setup_inputs


def setup_inputs(seed=0):
    import zlib

    import numpy as np

    out = dict(_drawn_inputs(seed))
    spreads = {'L1_conv_b_qkv': (0.0, 0.1), 'L1_conv_b_proj': (0.0, 0.622)}
    factors = {'L0_conv_gn_w': 8.0, 'L0_conv_proj_b': 5.422}
    for name, (base, spread) in spreads.items():
        noise = np.random.default_rng([zlib.crc32(name.encode()), seed]).standard_normal(out[name].shape)
        drawn = base * np.exp(spread * noise) if base else spread * noise
        out[name] = jnp.asarray(drawn.astype(out[name].dtype))
    for name, factor in factors.items():
        out[name] = (out[name] * factor).astype(out[name].dtype)
    return out
```

```python
from contextlib import ExitStack

import concourse.bass as bass
from concourse import mybir

F32 = mybir.dt.float32
F32R = mybir.dt.float32r
ALU = mybir.AluOpType
ACT = mybir.ActivationFunctionType
AX_X = mybir.AxisListType.X

P = 128
LAYERS = 2
HEADS = 8
BANK = 512
GROUPS = 32
EPS = 1e-6
HI, LO = 0, 1
SLOTS = 16

Q_SLOTS = (5, 6)
K_SLOTS = (9, 10)
NATQ_SLOT = 7
NATK_SLOT = 11
O_SLOT = 9
PROJ_SLOTS = (13, 14)
NORM_PAIR = 2


def head_of(u):
    return u % 2


def group_banks():
    order = []
    for p in range(4):
        for u in range(SLOTS):
            if u % 4 == 3:
                order.append((p, "pv", 0, u // 4))
            if u % 4 == 0 and u > 0:
                order.append((p, "pv", 1, u // 4 - 1))
            if u == 0:
                order += [(p, "vt", 0), (p, "vt", 1)]
            if u in Q_SLOTS:
                order.append((p, "q", Q_SLOTS.index(u)))
            if u in K_SLOTS:
                order.append((p, "k", K_SLOTS.index(u)))
            if u in PROJ_SLOTS:
                first = 2 * PROJ_SLOTS.index(u)
                order += [(p, "proj", 0, first), (p, "proj", 0, first + 1)]
            if p == NORM_PAIR and u == 11:
                order.append((p, "mean"))
            if p == NORM_PAIR and u == 12:
                order.append((p, "var"))
        order += [(p, "v", 0), (p, "pv", 1, 3), (p, "v", 1)]
        order += [(p, "proj", 1, c) for c in range(4)]
    assert len(order) % 2 == 0
    return {key: n % 2 for n, key in enumerate(order)}


def build(nc, x, w, b, gn, pb, y):
    IMAGES, C, T = x.shape
    KC = C // P
    PAIRS = HEADS // 2
    D = C // HEADS
    SCALE = float(D) ** -0.5
    HALF = T // 2
    NC8 = T // P
    TURNS = LAYERS * IMAGES
    assert D == 64 and KC == 4 and PAIRS == 4 and HALF == BANK and NC8 * 2 == SLOTS

    with ExitStack() as ctx:
        def sb(name, shape, dt=F32):
            return ctx.enter_context(nc.sbuf_tensor(name, shape, dt))

        def sem(name):
            return ctx.enter_context(nc.semaphore(name))

        split_w = nc.dram_tensor("split_w", (LAYERS * PAIRS, P, 4, 2, 512), F32, kind="Internal").ap()

        xs = sb("xs", [P, 2, KC, T], F32R)
        raw = sb("raw", [P, KC, T])
        acc = sb("acc", [P, KC, T])
        wt = [sb(f"w_{n}", [P, 2, KC, P], F32R) for n in "qkv"]
        wp = sb("w_proj", [P, 2, KC, P], F32R)
        nat = sb("nat", [P, 2, T], F32R)
        qst = sb("q_stack", [P, 2, 2, T], F32R)
        khi = sb("k_hi", [P, 2, 2, T], F32R)
        klo = sb("k_lo", [P, 2, 2, T], F32R)
        vt = sb("v_channels", [P, T])
        vst = sb("v_pixels", [P, NC8, 4, D], F32R)
        probs = [sb(f"probs{i}", [P, T]) for i in range(4)]
        pt = [sb(f"probs_t{n}", [P, 2, NC8, 256], F32R) for n in ("hi", "lo")]
        o_half = sb("o_half", [P, 256])
        o_sum = sb("o_sum", [P, BANK])
        o_hi = sb("o_hi", [P, BANK], F32R)
        o_lo = sb("o_lo", [P, BANK], F32R)
        ident = sb("ident", [P, P])
        averager = sb("averager", [P, P])
        bias = sb("bias", [P, LAYERS * PAIRS, 3])
        gnw = sb("gnw", [P, LAYERS, KC])
        gnb = sb("gnb", [P, LAYERS, KC])
        gate = sb("gate", [P, LAYERS, 2])
        oscale = sb("oscale", [P, LAYERS])
        obias = sb("obias", [P, LAYERS, KC])
        zero = sb("zero", [P, 1])
        stats = sb("stats", [P, KC, 2, 6])
        moments = sb("moments", [P, KC, 2])
        gmean = sb("gmean", [P, KC])
        cvar = sb("cvar", [P, KC])
        rstd = sb("rstd", [P, KC])
        power = sb("power", [P, KC])
        coef_a0 = sb("coef_a0", [P, KC])
        coef_a = sb("coef_a", [P, KC])
        coef_b = sb("coef_b", [P, KC])
        neg_max = sb("neg_max", [P, 2])
        row_sum = sb("row_sum", [P, 2])
        row_inv = sb("row_inv", [P, 4])

        ps_s = [ctx.enter_context(nc.psum_tensor(f"ps_scores{i}", [P, T], F32)) for i in range(2)]
        ps_t = ctx.enter_context(nc.psum_tensor("ps_transposed", [P, T], F32))
        ps_m = [ctx.enter_context(nc.psum_tensor(f"ps_small{i}", [P, BANK], F32)) for i in range(2)]

        scores_ready = sem("scores_ready")
        scores_free = sem("scores_free")
        max_ready = sem("max_ready")
        exp_done = sem("exp_done")
        inv_ready = sem("inv_ready")
        probs_ready = sem("probs_ready")
        t_ready = sem("t_ready")
        t_hi = sem("t_hi")
        t_lo = sem("t_lo")
        small_free = [sem(f"small_free{i}") for i in range(2)]
        to_act = sem("to_act")
        to_dve = sem("to_dve")
        hi_out = sem("hi_out")
        q_out = sem("q_out")
        k_out = sem("k_out")
        q_stacked = sem("q_stacked")
        k_stacked = sem("k_stacked")
        w_used = sem("w_used")
        w_ready = [sem(f"w_ready_{n}") for n in "qkv"]
        wp_used = sem("wp_used")
        wp_ready = sem("wp_ready")
        o_out = sem("o_out")
        o_split = sem("o_split")
        o_hi_done = sem("o_hi_done")
        acc_ready = sem("acc_ready")
        acc_done = sem("acc_done")
        out_ready = sem("out_ready")
        stored = sem("stored")
        copied = sem("copied")
        raw_ready = sem("raw_ready")
        raw_used = sem("raw_used")
        dve_own = sem("dve_own")
        moments_ready = sem("moments_ready")
        var_ready = sem("var_ready")
        rstd_ready = sem("rstd_ready")
        coef_ready = sem("coef_ready")
        xn_ready = sem("xn_ready")
        x_hi = sem("x_hi")
        x_split = sem("x_split")
        params = sem("params")
        const_ready = sem("const_ready")
        pool_own = sem("pool_own")
        w_raw = [sem(f"w_raw{i}") for i in range(2)]
        w_hi = sem("w_hi")
        w_lo = sem("w_lo")
        w_stored = sem("w_stored")

        bank = group_banks()
        w_slots = [probs[0], probs[1], probs[2], probs[3]]
        LP = LAYERS * PAIRS

        def pt_flat(part, s):
            return pt[part][:, s].rearrange("p c q -> p (c q)")

        block = ctx.enter_context(nc.Block())

        @block.sync
        def _(sp):
            sp.dma_start(bias[:], b.rearrange("t p j -> p t j")).then_inc(params, 16)
            sp.dma_start(gnw[:, 0, :], gn[0]).then_inc(params, 16)
            sp.dma_start(gnb[:, 0, :], gn[1]).then_inc(params, 16)
            sp.dma_start(obias[:], pb.rearrange("l p c -> p l c")).then_inc(params, 16)
            for t in range(2):
                for h in range(2):
                    sp.dma_start(probs[2 * t + h][:], w[t, :, 2 * h:2 * h + 2, :].rearrange("p s n -> p (s n)")).then_inc(w_raw[t], 16)
            sp.dma_start(raw[:], x[0].rearrange("(c p) t -> p c t", p=P)).then_inc(raw_ready, 16)
            for t in range(LP):
                s = t % 2
                sp.wait_ge(w_lo, 1).then_inc(w_lo, -1)
                for part in (HI, LO):
                    sp.dma_start(split_w[t, :, :, part, :], pt_flat(part, s).bitcast(F32).rearrange("p (s n) -> p s n", s=4)).then_inc(w_stored, 16)
                if t + 2 < LP:
                    for h in range(2):
                        sp.dma_start(probs[2 * s + h][:], w[t + 2, :, 2 * h:2 * h + 2, :].rearrange("p s n -> p (s n)")).then_inc(w_raw[s], 16)
                sp.wait_ge(w_stored, 32 * (t + 1))
                if t == 0:
                    for j in range(3):
                        sp.dma_start(wt[j][:].bitcast(F32), split_w[0, :, j].rearrange("p a (k m) -> p a k m", k=KC)).then_inc(w_ready[j], 16)
                    sp.dma_start(wp[:].bitcast(F32), split_w[0, :, 3].rearrange("p a (k m) -> p a k m", k=KC)).then_inc(wp_ready, 16)
            sp.dma_start(acc[:], x[0].rearrange("(c p) t -> p c t", p=P)).then_inc(acc_ready, 16)
            sp.dma_start(y[0:IMAGES].rearrange("i (a c) t -> (i a) (c t)", a=16), x.rearrange("i (a c) t -> (i a) (c t)", a=16)).then_inc(copied, 16)

            def stack_q(par):
                sp.wait_ge(q_out, 1).then_inc(q_out, -1)
                for h in range(2):
                    for part in (HI, LO):
                        sp.dma_start(qst[part * D:part * D + D, par, h, :].bitcast(F32), nat[h * D:h * D + D, part, :].bitcast(F32)).then_inc(q_stacked, 16)

            def stack_k(par):
                sp.wait_ge(k_out, 1).then_inc(k_out, -1)
                for h in range(2):
                    for dst, part in ((khi, HI), (klo, LO)):
                        for up in range(2):
                            sp.dma_start(dst[up * D:up * D + D, par, h, :].bitcast(F32), nat[h * D:h * D + D, part, :].bitcast(F32)).then_inc(k_stacked, 16)

            def load_w(j, t):
                sp.wait_ge(w_used, 1).then_inc(w_used, -1)
                sp.dma_start(wt[j][:].bitcast(F32), split_w[bass.ds(t, 1), :, j].rearrange("o p a (k m) -> (o p) a k m", k=KC)).then_inc(w_ready[j], 16)

            stack_q(0)
            load_w(0, 1)
            stack_k(0)
            load_w(1, 1)
            load_w(2, 1)
            with sp.Fori(0, TURNS) as i:
                layer = i // IMAGES
                layer_next = (i + 1) // IMAGES % LAYERS
                for p in range(PAIRS):
                    if p == 1:
                        sp.wait_ge(copied, 16)
                        sp.wait_ge(raw_used, KC).then_inc(raw_used, -KC)
                        sp.dma_start(raw[:], y[bass.ds(i + 1, 1)].rearrange("o (c p) t -> p (o c) t", p=P)).then_inc(raw_ready, 16)
                    after = layer * PAIRS + p + 2 if p < 2 else layer_next * PAIRS + p - 2
                    stack_q((p + 1) % 2)
                    load_w(0, after)
                    stack_k((p + 1) % 2)
                    load_w(1, after)
                    load_w(2, after)
                    follows = layer * PAIRS + p + 1 if p < 3 else layer_next * PAIRS
                    sp.wait_ge(wp_used, 1).then_inc(wp_used, -1)
                    sp.dma_start(wp[:].bitcast(F32), split_w[bass.ds(follows, 1), :, 3].rearrange("o p a (k m) -> (o p) a k m", k=KC)).then_inc(wp_ready, 16)
                for c in range(KC):
                    sp.wait_ge(out_ready, 1).then_inc(out_ready, -1)
                    sp.dma_start(y[bass.ds(i + IMAGES, 1), c * P:(c + 1) * P, :].rearrange("o p t -> (o p) t"), acc[:, c, :]).then_inc(stored, 16)
                sp.wait_ge(stored, KC * 16).then_inc(stored, -KC * 16)
                sp.dma_start(acc[:], y[bass.ds(i + 1, 1)].rearrange("o (c p) t -> p (o c) t", p=P)).then_inc(acc_ready, 16)
            sp.wait_ge(acc_ready, 16)
            sp.wait_ge(wp_ready, 16)
            for j in range(3):
                sp.wait_ge(w_ready[j], 16)

        @block.tensor
        def _(pe):
            def start_small(key):
                n = bank[key]
                pe.wait_ge(small_free[n], 1).then_inc(small_free[n], -1)
                return ps_m[n]

            def project_in(j, key, half):
                if half == 0:
                    pe.wait_ge(w_ready[j], 16).then_inc(w_ready[j], -16)
                out = start_small(key)
                cols = slice(half * HALF, (half + 1) * HALF)
                terms = [(wl, xl, k) for k in range(KC) for wl, xl in ((HI, HI), (HI, LO), (LO, HI))]
                for n, (wl, xl, k) in enumerate(terms):
                    last = nc.tensor.matmul(out[:], wt[j][:, wl, k, :], xs[:, xl, k, cols], start=n == 0, stop=n == len(terms) - 1)
                last.then_inc(to_act, 1)

            def scores(u, par):
                pe.wait_ge(scores_free, 1).then_inc(scores_free, -1)
                h, qb = head_of(u), u // 2
                for half in range(2):
                    cols = slice(half * HALF, (half + 1) * HALF)
                    for n, k in enumerate((khi, klo)):
                        last = nc.tensor.matmul(ps_s[u % 2][:, cols], qst[:, par, h, qb * P:(qb + 1) * P], k[:, par, h, cols], start=n == 0, stop=n == 1)
                last.then_inc(scores_ready, 1)

            def transposes(u):
                pe.wait_ge(probs_ready, 1).then_inc(probs_ready, -1)
                for c in range(NC8):
                    last = nc.tensor.transpose(ps_t[:, c * P:(c + 1) * P], probs[u % 4][:, c * P:(c + 1) * P], ident[:])
                last.then_inc(t_ready, 1)

            def attend(key, h):
                out = start_small(key)
                for c in range(NC8):
                    for part in (HI, LO):
                        last = nc.tensor.matmul(out[:, 0:256], vst[:, c, 2 * h:2 * h + 2, :].rearrange("p a d -> p (a d)"), pt[part][:, h, c, :],
                                                start=c == 0 and part == HI, stop=c == NC8 - 1 and part == LO)
                last.then_inc(to_act, 1)

            def turn_v(key, half):
                out = start_small(key)
                for c in range(4):
                    last = nc.tensor.transpose(out[:, c * P:(c + 1) * P], vt[:, (4 * half + c) * P:(4 * half + c + 1) * P], ident[:])
                last.then_inc(to_act, 1)

            def project_out(key, c):
                out = start_small(key)
                for n, (wl, o) in enumerate(((HI, o_hi), (HI, o_lo), (LO, o_hi))):
                    last = nc.tensor.matmul(out[:], wp[:, wl, c, :], o[:], start=n == 0, stop=n == 2)
                last.then_inc(to_dve, 1)

            def group_mean(key):
                pe.wait_ge(moments_ready, 1).then_inc(moments_ready, -1)
                out = start_small(key)
                nc.tensor.matmul(out[:, 0:2 * KC], averager[:], moments[:].rearrange("p c s -> p (c s)"), start=True, stop=True).then_inc(to_dve, 1)

            def group_var(key):
                pe.wait_ge(moments_ready, 1).then_inc(moments_ready, -1)
                out = start_small(key)
                nc.tensor.matmul(out[:, 0:KC], averager[:], cvar[:], start=True, stop=True).then_inc(to_dve, 1)

            pe.wait_ge(const_ready, 2)
            group_mean((NORM_PAIR, "mean"))
            group_var((NORM_PAIR, "var"))
            pe.wait_ge(x_split, KC).then_inc(x_split, -KC)
            for half in range(2):
                project_in(0, (0, "q", half), half)
            pe.wait_ge(small_free[0], 1)
            pe.wait_ge(small_free[1], 1)
            pe.sem_inc(q_out, 1)
            for half in range(2):
                project_in(1, (0, "k", half), half)
            pe.wait_ge(small_free[0], 1)
            pe.wait_ge(small_free[1], 1)
            pe.sem_inc(k_out, 1)
            for half in range(2):
                project_in(2, (0, "v", half), half)
            pe.wait_ge(k_stacked, 128).then_inc(k_stacked, -128)
            scores(0, 0)
            scores(1, 0)

            with pe.Fori(0, TURNS):
                for p in range(PAIRS):
                    par = p % 2
                    for u in range(SLOTS):
                        if u > 0:
                            pe.wait_ge(t_lo, 1).then_inc(t_lo, -1)
                        transposes(u)
                        if u == NATQ_SLOT:
                            pe.wait_ge(small_free[0], 1)
                            pe.wait_ge(small_free[1], 1)
                            pe.sem_inc(q_out, 1)
                        if u == NATK_SLOT:
                            pe.wait_ge(small_free[0], 1)
                            pe.wait_ge(small_free[1], 1)
                            pe.sem_inc(k_out, 1)
                        if u % 4 == 3:
                            attend((p, "pv", 0, u // 4), 0)
                        if u % 4 == 0 and u > 0:
                            attend((p, "pv", 1, u // 4 - 1), 1)
                        if u < SLOTS - 2:
                            scores(u + 2, par)
                        else:
                            if u == SLOTS - 2:
                                pe.wait_ge(k_stacked, 128).then_inc(k_stacked, -128)
                            scores(u + 2 - SLOTS, 1 - par)
                        if u == 0:
                            turn_v((p, "vt", 0), 0)
                            turn_v((p, "vt", 1), 1)
                        if u == Q_SLOTS[0] and p == PAIRS - 1:
                            pe.wait_ge(x_split, KC).then_inc(x_split, -KC)
                        if u in Q_SLOTS:
                            project_in(0, (p, "q", Q_SLOTS.index(u)), Q_SLOTS.index(u))
                        if u == O_SLOT:
                            pe.wait_ge(small_free[bank[(p, "pv", 1, 1)]], 1)
                            pe.sem_inc(o_out, 1)
                        if u in K_SLOTS:
                            project_in(1, (p, "k", K_SLOTS.index(u)), K_SLOTS.index(u))
                        if u in PROJ_SLOTS:
                            first = 2 * PROJ_SLOTS.index(u)
                            if first == 0:
                                pe.wait_ge(wp_ready, 16).then_inc(wp_ready, -16)
                                pe.wait_ge(o_split, 1).then_inc(o_split, -1)
                            project_out((p, "proj", 0, first), first)
                            project_out((p, "proj", 0, first + 1), first + 1)
                        if p == NORM_PAIR and u == 11:
                            group_mean((p, "mean"))
                        if p == NORM_PAIR and u == 12:
                            group_var((p, "var"))
                    project_in(2, (p, "v", 0), 0)
                    pe.wait_ge(t_lo, 1).then_inc(t_lo, -1)
                    attend((p, "pv", 1, 3), 1)
                    project_in(2, (p, "v", 1), 1)
                    pe.wait_ge(small_free[bank[(p, "pv", 1, 3)]], 1)
                    pe.sem_inc(o_out, 1)
                    pe.wait_ge(o_split, 1).then_inc(o_split, -1)
                    for c in range(KC):
                        project_out((p, "proj", 1, c), c)
                pe.wait_ge(small_free[0], 1)
                pe.wait_ge(small_free[1], 1)
                pe.sem_inc(acc_done, 1)

        @block.scalar
        def _(act):
            def exps(u):
                act.wait_ge(max_ready, 1).then_inc(max_ready, -1)
                nc.scalar.activation(probs[u % 4][:], ps_s[u % 2][:], ACT.Exp, bias=neg_max[:, u % 2:u % 2 + 1],
                                     accum_out=row_sum[:, u % 2:u % 2 + 1]).then_inc(exp_done, 1)

            def round_qk(p, name, half, bias_ap):
                act.wait_ge(to_act, 1).then_inc(to_act, -1)
                nc.scalar.activation(nat[:, HI, half * HALF:(half + 1) * HALF], ps_m[bank[(p, name, half)]][:], ACT.Identity, bias=bias_ap).then_inc(hi_out, 1)
                if half == 1:
                    act.sem_inc(w_used, 1)

            def add_bias_v(p, half, bias_ap):
                act.wait_ge(to_act, 1).then_inc(to_act, -1)
                n = bank[(p, "v", half)]
                nc.scalar.activation(vt[:, half * HALF:(half + 1) * HALF], ps_m[n][:], ACT.Identity, bias=bias_ap).then_inc(small_free[n], 1)
                if half == 1:
                    act.sem_inc(w_used, 1)

            def far_half(p, h, qt):
                act.wait_ge(to_act, 1).then_inc(to_act, -1)
                nc.scalar.activation(o_half[h * D:(h + 1) * D, :], ps_m[bank[(p, "pv", h, qt)]][(1 - h) * D:(2 - h) * D, 0:256], ACT.Copy).then_inc(hi_out, 1)

            def normalise(c):
                nc.scalar.activation(raw[:, c, :], raw[:, c, :], ACT.Identity, bias=coef_b[:, c:c + 1], scale=coef_a[:, c:c + 1]).then_inc(xn_ready, 1)

            for t in range(LP):
                act.wait_ge(w_raw[t % 2], 32 * (t // 2 + 1))
                if t >= 2:
                    act.wait_ge(w_stored, 32 * (t - 1))
                flat = pt_flat(HI, t % 2)
                nc.scalar.activation(flat[:, 0:512], probs[2 * (t % 2)][:, 0:512], ACT.Copy, scale=SCALE)
                nc.scalar.activation(flat[:, 512:1024], probs[2 * (t % 2)][:, 512:1024], ACT.Copy)
                nc.scalar.activation(flat[:, 1024:2048], probs[2 * (t % 2) + 1][:], ACT.Copy).then_inc(w_hi, 1)
            act.wait_ge(coef_ready, 1).then_inc(coef_ready, -1)
            for c in range(KC):
                normalise(c)
            for half in range(2):
                round_qk(0, "q", half, bias[:, 0, 0:1])
            act.wait_ge(q_stacked, 64).then_inc(q_stacked, -64)
            for half in range(2):
                round_qk(0, "k", half, bias[:, 0, 1:2])
            for half in range(2):
                add_bias_v(0, half, bias[:, 0, 2:3])
            exps(0)
            exps(1)

            with act.Fori(0, TURNS) as i:
                layer = i // IMAGES
                layer_next = (i + 1) // IMAGES % LAYERS
                for p in range(PAIRS):
                    pair = layer * PAIRS + p + 1 if p < 3 else layer_next * PAIRS

                    def bias_of(j):
                        return bias[:, bass.ds(pair, 1), j:j + 1].rearrange("p o j -> p (o j)")

                    for u in range(SLOTS):
                        h, qb = head_of(u), u // 2
                        act.wait_ge(t_ready, 1).then_inc(t_ready, -1)
                        nc.scalar.activation(pt[HI][:, h, :, (qb % 2) * P:(qb % 2 + 1) * P], ps_t[:].rearrange("p (c q) -> p c q", q=P), ACT.Copy).then_inc(t_hi, 1)
                        if u % 4 == 3:
                            far_half(p, 0, u // 4)
                        if u % 4 == 0 and u > 0:
                            far_half(p, 1, u // 4 - 1)
                        exps((u + 2) % SLOTS)
                        if u == 0:
                            for half in range(2):
                                act.wait_ge(to_act, 1).then_inc(to_act, -1)
                                nc.scalar.activation(vst[:, 4 * half:4 * half + 4, 0:4:3, :], ps_m[bank[(p, "vt", half)]][:].rearrange("p (c h d) -> p c h d", c=4, h=2), ACT.Copy).then_inc(hi_out, 1)
                        if u in Q_SLOTS:
                            round_qk(p, "q", Q_SLOTS.index(u), bias_of(0))
                        if u in K_SLOTS:
                            if u == K_SLOTS[0]:
                                act.wait_ge(q_stacked, 64).then_inc(q_stacked, -64)
                            round_qk(p, "k", K_SLOTS.index(u), bias_of(1))
                        if p == NORM_PAIR and u == 14:
                            act.wait_ge(coef_ready, 1).then_inc(coef_ready, -1)
                            normalise(0)
                            normalise(1)
                        if p == NORM_PAIR and u == 15:
                            normalise(2)
                            normalise(3)
                    add_bias_v(p, 0, bias_of(2))
                    far_half(p, 1, 3)
                    add_bias_v(p, 1, bias_of(2))
                act.wait_ge(acc_done, 1).then_inc(acc_done, -1)
                for c in range(KC):
                    nc.scalar.activation(acc[:, c, :], acc[:, c, :], ACT.Identity, bias=obias[:, bass.ds(layer, 1), c:c + 1].rearrange("p o c -> p (o c)"),
                                         scale=oscale[:, bass.ds(layer, 1)]).then_inc(out_ready, 1)

        @block.vector
        def _(dve):
            def own(instruction):
                instruction.then_inc(dve_own, 1)
                dve.wait_ge(dve_own, 1).then_inc(dve_own, -1)

            def maxima(u):
                dve.wait_ge(scores_ready, 1).then_inc(scores_ready, -1)
                nc.vector.tensor_reduce(neg_max[:, u % 2:u % 2 + 1], ps_s[u % 2][:], AX_X, ALU.max, negate=True).then_inc(max_ready, 1)

            def inverse(u):
                dve.wait_ge(exp_done, 1).then_inc(exp_done, -1)
                dve.sem_inc(scores_free, 1)
                nc.vector.reciprocal(row_inv[:, u % 4:u % 4 + 1], row_sum[:, u % 2:u % 2 + 1]).then_inc(inv_ready, 1)

            def rest_qk(p, name, half, bias_ap):
                dve.wait_ge(hi_out, 1).then_inc(hi_out, -1)
                n = bank[(p, name, half)]
                cols = slice(half * HALF, (half + 1) * HALF)
                nc.vector.scalar_tensor_tensor(out=nat[:, LO, cols], in0=ps_m[n][:], scalar=bias_ap, in1=nat[:, HI, cols].bitcast(F32),
                                               op0=ALU.add, op1=ALU.subtract).then_inc(small_free[n], 1)

            def sum_halves(p, h, qt):
                dve.wait_ge(hi_out, 1).then_inc(hi_out, -1)
                n = bank[(p, "pv", h, qt)]
                rows = slice(h * D, (h + 1) * D)
                nc.vector.tensor_tensor(o_sum[rows, (qt % 2) * 256:(qt % 2 + 1) * 256], ps_m[n][rows, 0:256], o_half[rows, :], ALU.add).then_inc(small_free[n], 1)

            def add_projection(p, half, c):
                dve.wait_ge(to_dve, 1).then_inc(to_dve, -1)
                n = bank[(p, "proj", half, c)]
                cols = slice(half * HALF, (half + 1) * HALF)
                nc.vector.tensor_tensor(acc[:, c, cols], ps_m[n][:], acc[:, c, cols], ALU.add).then_inc(small_free[n], 1)

            def channel_stats(n):
                c, half = n // 2, n % 2
                if n == 0:
                    dve.wait_ge(raw_ready, 16).then_inc(raw_ready, -16)
                own(nc.vector.bn_stats(stats[:, c, half, :], raw[:, c, half * HALF:(half + 1) * HALF]))

            def channel_moments():
                for c in range(KC):
                    last = nc.vector.bn_aggr(moments[:, c, :], stats[:, c])
                last.then_inc(moments_ready, 1)

            def group_means():
                dve.wait_ge(to_dve, 1).then_inc(to_dve, -1)
                n = bank[(NORM_PAIR, "mean")]
                own(nc.vector.tensor_copy(gmean[:], ps_m[n][:, 0:2 * KC].rearrange("p (c s) -> p c s", s=2)[:, :, 0]))
                dve.sem_inc(small_free[n], 1)
                own(nc.vector.tensor_tensor(cvar[:], moments[:, :, 0], gmean[:], ALU.subtract))
                own(nc.vector.tensor_tensor(cvar[:], cvar[:], cvar[:], ALU.mult))
                nc.vector.tensor_tensor(cvar[:], cvar[:], moments[:, :, 1], ALU.add).then_inc(moments_ready, 1)

            def group_vars():
                dve.wait_ge(to_dve, 1).then_inc(to_dve, -1)
                n = bank[(NORM_PAIR, "var")]
                own(nc.vector.tensor_scalar(rstd[:], ps_m[n][:, 0:KC], EPS, None, ALU.add))
                dve.sem_inc(small_free[n], 1)
                dve.sem_inc(var_ready, 1)

            def coefficients(at):
                dve.wait_ge(rstd_ready, 1).then_inc(rstd_ready, -1)
                w_ap = gnw[:, bass.ds(at, 1), :].rearrange("p o c -> p (o c)")
                b_ap = gnb[:, bass.ds(at, 1), :].rearrange("p o c -> p (o c)")
                on = gate[:, bass.ds(at, 1), 0:1].rearrange("p o c -> p (o c)")
                off = gate[:, bass.ds(at, 1), 1:2].rearrange("p o c -> p (o c)")
                own(nc.vector.tensor_tensor(coef_a0[:], rstd[:], w_ap, ALU.mult))
                own(nc.vector.tensor_tensor(coef_b[:], gmean[:], coef_a0[:], ALU.mult))
                own(nc.vector.tensor_tensor(coef_b[:], b_ap, coef_b[:], ALU.subtract))
                own(nc.vector.tensor_scalar(coef_b[:], coef_b[:], on, None, ALU.mult))
                nc.vector.tensor_scalar(coef_a[:], coef_a0[:], on, off, ALU.mult, ALU.add).then_inc(coef_ready, 1)

            def round_x(c):
                dve.wait_ge(xn_ready, 1).then_inc(xn_ready, -1)
                nc.vector.tensor_copy(xs[:, HI, c, :], raw[:, c, :]).then_inc(x_hi, 1)

            nc.vector.memset(gate[:, 0, 0:1], 1.0)
            nc.vector.memset(gate[:, 0, 1:2], 0.0)
            nc.vector.memset(gate[:, 1, 0:1], 0.0)
            nc.vector.memset(gate[:, 1, 1:2], 1.0)
            nc.vector.memset(gnw[:, 1, :], 0.0)
            nc.vector.memset(gnb[:, 1, :], 0.0)
            nc.vector.memset(oscale[:, 0:1], 2.0 ** -0.5)
            own(nc.vector.memset(oscale[:, 1:2], 1.0))
            dve.wait_ge(params, 64)
            own(nc.vector.tensor_scalar(bias[:, :, 0], bias[:, :, 0], SCALE, None, ALU.mult))
            own(nc.vector.tensor_scalar(obias[:, 0, :], obias[:, 0, :], oscale[:, 0:1], None, ALU.mult))
            for n in range(2):
                dve.sem_inc(small_free[n], 1)
            dve.sem_inc(scores_free, 2)
            for t in range(LP):
                dve.wait_ge(w_hi, 1).then_inc(w_hi, -1)
                hi, lo = pt_flat(HI, t % 2).bitcast(F32), pt_flat(LO, t % 2)
                if t >= 2:
                    dve.wait_ge(w_stored, 32 * (t - 1))
                nc.vector.scalar_tensor_tensor(out=lo[:, 0:512], in0=probs[2 * (t % 2)][:, 0:512], scalar=SCALE, in1=hi[:, 0:512], op0=ALU.mult, op1=ALU.subtract)
                nc.vector.tensor_tensor(lo[:, 512:1024], probs[2 * (t % 2)][:, 512:1024], hi[:, 512:1024], ALU.subtract)
                nc.vector.tensor_tensor(lo[:, 1024:2048], probs[2 * (t % 2) + 1][:], hi[:, 1024:2048], ALU.subtract).then_inc(w_lo, 1)
            for n in range(2 * KC):
                channel_stats(n)
            channel_moments()
            group_means()
            group_vars()
            coefficients(0)
            for c in range(KC):
                round_x(c)
            for half in range(2):
                rest_qk(0, "q", half, bias[:, 0, 0:1])
            for half in range(2):
                rest_qk(0, "k", half, bias[:, 0, 1:2])
            maxima(0)
            maxima(1)
            inverse(0)

            with dve.Fori(0, TURNS) as i:
                layer = i // IMAGES
                layer_next = (i + 1) // IMAGES % LAYERS
                for p in range(PAIRS):
                    pair = layer * PAIRS + p + 1 if p < 3 else layer_next * PAIRS

                    def bias_of(j):
                        return bias[:, bass.ds(pair, 1), j:j + 1].rearrange("p o j -> p (o j)")

                    for u in range(SLOTS):
                        h, qb = head_of(u), u // 2
                        inverse((u + 1) % SLOTS)
                        dve.wait_ge(t_hi, 1).then_inc(t_hi, -1)
                        cols = slice((qb % 2) * P, (qb % 2 + 1) * P)
                        nc.vector.tensor_tensor(pt[LO][:, h, :, cols], ps_t[:].rearrange("p (c q) -> p c q", q=P), pt[HI][:, h, :, cols].bitcast(F32), ALU.subtract).then_inc(t_lo, 1)
                        if u % 4 == 3:
                            sum_halves(p, 0, u // 4)
                        if u % 4 == 0 and u > 0:
                            sum_halves(p, 1, u // 4 - 1)
                        maxima((u + 2) % SLOTS)
                        if u == 0:
                            for half in range(2):
                                dve.wait_ge(hi_out, 1).then_inc(hi_out, -1)
                                n = bank[(p, "vt", half)]
                                nc.vector.tensor_tensor(vst[:, 4 * half:4 * half + 4, 1:3, :], ps_m[n][:].rearrange("p (c h d) -> p c h d", c=4, h=2),
                                                        vst[:, 4 * half:4 * half + 4, 0:4:3, :].bitcast(F32), ALU.subtract).then_inc(small_free[n], 1)
                        if u in Q_SLOTS:
                            rest_qk(p, "q", Q_SLOTS.index(u), bias_of(0))
                        if u in K_SLOTS:
                            rest_qk(p, "k", K_SLOTS.index(u), bias_of(1))
                        if u in PROJ_SLOTS:
                            first = 2 * PROJ_SLOTS.index(u)
                            if first == 0 and p == 0:
                                dve.wait_ge(acc_ready, 16).then_inc(acc_ready, -16)
                            add_projection(p, 0, first)
                            add_projection(p, 0, first + 1)
                        if p == NORM_PAIR:
                            if u < 8:
                                channel_stats(u)
                            if u == 8:
                                channel_moments()
                            if u == 11:
                                group_means()
                            if u == 12:
                                group_vars()
                            if u == 13:
                                coefficients(layer_next)
                        if p == PAIRS - 1 and 1 <= u <= KC:
                            round_x(u - 1)
                    sum_halves(p, 1, 3)
                    for c in range(KC):
                        add_projection(p, 1, c)
                    dve.sem_inc(wp_used, 1)

        @block.gpsimd
        def _(pool):
            def own(instruction):
                instruction.then_inc(pool_own, 1)
                pool.wait_ge(pool_own, 1).then_inc(pool_own, -1)

            def scale_probs(u):
                pool.wait_ge(inv_ready, 1).then_inc(inv_ready, -1)
                nc.gpsimd.tensor_tensor(probs[u % 4][:], probs[u % 4][:], row_inv[:, u % 4:u % 4 + 1].to_broadcast([P, T]), ALU.mult).then_inc(probs_ready, 1)

            def split_o():
                pool.wait_ge(o_out, 1).then_inc(o_out, -1)
                own(nc.gpsimd.tensor_tensor(o_hi[:], o_sum[:], zero[:, 0:1].to_broadcast([P, BANK]), ALU.add))
                nc.gpsimd.tensor_tensor(o_lo[:], o_sum[:], o_hi[:].bitcast(F32), ALU.subtract).then_inc(o_split, 1)

            def rest_x(c):
                pool.wait_ge(x_hi, 1).then_inc(x_hi, -1)
                own(nc.gpsimd.tensor_tensor(xs[:, LO, c, :], raw[:, c, :], xs[:, HI, c, :].bitcast(F32), ALU.subtract))
                pool.sem_inc(x_split, 1)
                pool.sem_inc(raw_used, 1)

            def inverse_root():
                pool.wait_ge(var_ready, 1).then_inc(var_ready, -1)
                nc.gpsimd.tensor_tensor(rstd[:], rstd[:], power[:], ALU.pow).then_inc(rstd_ready, 1)

            own(nc.gpsimd.memset(ident[:], 0.0))
            nc.gpsimd.affine_select(out=ident[:], in_=ident[:], compare_op=ALU.not_equal, fill=1.0, base=0,
                                    pattern=[[-1, P]], channel_multiplier=1).then_inc(const_ready, 1)
            per_group = C // GROUPS
            own(nc.gpsimd.memset(averager[:], 1.0 / per_group))
            by_group = averager[:].rearrange("p (g m) -> p g m", m=per_group)
            own(nc.gpsimd.affine_select(out=by_group, in_=by_group, compare_op=ALU.is_ge, fill=0.0, base=0,
                                        pattern=[[-per_group, P // per_group], [0, per_group]], channel_multiplier=1))
            nc.gpsimd.affine_select(out=by_group, in_=by_group, compare_op=ALU.is_ge, fill=0.0, base=per_group - 1,
                                    pattern=[[per_group, P // per_group], [0, per_group]], channel_multiplier=-1).then_inc(const_ready, 1)
            nc.gpsimd.memset(zero[:], 0.0)
            own(nc.gpsimd.memset(power[:], -0.5))
            inverse_root()
            for c in range(KC):
                rest_x(c)
            scale_probs(0)
            with pool.Fori(0, TURNS):
                for p in range(PAIRS):
                    for u in range(SLOTS):
                        scale_probs((u + 1) % SLOTS)
                        if u == O_SLOT:
                            split_o()
                        if p == NORM_PAIR and u == 12:
                            inverse_root()
                        if p == PAIRS - 1 and 1 <= u <= KC:
                            rest_x(u - 1)
                    split_o()


def kernel(x, L0_conv_gn_w, L0_conv_gn_b, L0_conv_qkv_w, L0_conv_qkv_b, L0_conv_proj_w, L0_conv_proj_b,
           L1_conv_w_qkv, L1_conv_b_qkv, L1_conv_w_proj, L1_conv_b_proj):
    import numpy as np
    import concourse.bacc as bacc
    from concourse.bass_utils import run_bass_kernel_spmd

    B, C, H, W = x.shape
    pairs, d = HEADS // 2, C // HEADS

    def lay_in(w_in, w_out):
        q = np.asarray(w_in).reshape(C // P, P, pairs, 2, 3, d).transpose(2, 1, 4, 0, 3, 5).reshape(pairs, P, 3, C)
        o = np.asarray(w_out).reshape(pairs, P, 1, C)
        return np.concatenate([q, o], 2)

    def lay_bias(v):
        return np.asarray(v).reshape(pairs, 2, 3, d).transpose(0, 1, 3, 2).reshape(pairs, P, 3)

    def lay_channels(v):
        return np.asarray(v).reshape(C // P, P).T

    arrays = {
        "x": np.asarray(x).reshape(B, C, H * W),
        "w": np.concatenate([lay_in(np.asarray(L0_conv_qkv_w).T, np.asarray(L0_conv_proj_w).T), lay_in(L1_conv_w_qkv, L1_conv_w_proj)]),
        "b": np.concatenate([lay_bias(L0_conv_qkv_b), lay_bias(L1_conv_b_qkv)]),
        "gn": np.stack([lay_channels(L0_conv_gn_w), lay_channels(L0_conv_gn_b)]),
        "pb": np.stack([lay_channels(L0_conv_proj_b), lay_channels(L1_conv_b_proj)]),
    }
    arrays = {k: np.ascontiguousarray(a) for k, a in arrays.items()}
    nc = bacc.Bacc("TRN2", target_bir_lowering=False, num_devices=1)
    aps = [nc.dram_tensor(n, a.shape, mybir.dt.from_np(a.dtype), kind="ExternalInput").ap() for n, a in arrays.items()]
    y = nc.dram_tensor("y", (3 * B, C, H * W), F32, kind="ExternalOutput").ap()
    build(nc, *aps, y)
    r = run_bass_kernel_spmd(nc, [arrays], core_ids=[0])
    return r.results[0]["y"][2 * B:].reshape(B, C, H, W)
```

```python
from contextlib import ExitStack

import concourse.bass as bass
from concourse import mybir

F32 = mybir.dt.float32
F32R = mybir.dt.float32r
ALU = mybir.AluOpType
ACT = mybir.ActivationFunctionType
AX_X = mybir.AxisListType.X

P = 128
LAYERS = 2
HEADS = 8
BANK = 512
GROUPS = 32
EPS = 1e-6
HI, LO = 0, 1
SLOTS = 16

NORM_PAIR = 2


def head_of(u):
    return u % 2


def schedule(p):
    slots = [[] for _ in range(SLOTS)]
    for u in range(SLOTS):
        if u % 4 == 3:
            slots[u].append(("pv", 0, u // 4))
        if u % 4 == 0:
            slots[u].append(("pv", 1, (u // 4 - 1) % 4))
    slots[0] += [("vt", 0), ("vt", 1)]
    slots[2] += [("proj", 1, c) for c in range(4)]
    if p < 3:
        fill = {1: [("q", 0)], 5: [("q", 1)], 6: [("v", 0)], 9: [("k", 0)], 10: [("k", 1)],
                13: [("proj", 0, c) for c in range(4)], 14: [("v", 1)]}
    else:
        fill = {5: [("q", 0)], 6: [("q", 1)], 9: [("k", 0)], 10: [("k", 1)],
                12: [("proj", 0, c) for c in range(4)], 13: [("v", 0)], 14: [("v", 1)]}
    for u, items in fill.items():
        slots[u] += items
    if p == NORM_PAIR:
        slots[11].append(("mean",))
        slots[12].append(("var",))
    return slots


def group_banks():
    order = [(p, *item) for p in range(4) for items in schedule(p) for item in items]
    assert len(order) % 2 == 0
    return {key: n % 2 for n, key in enumerate(order)}


def q_out_slot(p):
    return 1 + max(u for u, items in enumerate(schedule(p)) if ("q", 1) in items)


K_OUT_SLOT = 11
O_OUT_SLOTS = {1: 1, 0: 9}


def build(nc, x, w, b, gn, pb, y):
    IMAGES, C, T = x.shape
    KC = C // P
    PAIRS = HEADS // 2
    D = C // HEADS
    SCALE = float(D) ** -0.5
    HALF = T // 2
    NC8 = T // P
    TURNS = LAYERS * IMAGES
    assert D == 64 and KC == 4 and PAIRS == 4 and HALF == BANK and NC8 * 2 == SLOTS

    with ExitStack() as ctx:
        def sb(name, shape, dt=F32):
            return ctx.enter_context(nc.sbuf_tensor(name, shape, dt))

        def sem(name):
            return ctx.enter_context(nc.semaphore(name))

        split_w = nc.dram_tensor("split_w", (LAYERS * PAIRS, P, 4, 2, 512), F32, kind="Internal").ap()

        xs = sb("xs", [P, 2, KC, T], F32R)
        raw = sb("raw", [P, KC, T])
        acc = sb("acc", [P, KC, T])
        wt = [sb(f"w_{n}", [P, 2, KC, P], F32R) for n in "qkv"]
        wp = sb("w_proj", [P, 2, KC, P], F32R)
        nat = sb("nat", [P, 2, T], F32R)
        qst = sb("q_stack", [P, 2, 2, T], F32R)
        khi = sb("k_hi", [P, 2, 2, T], F32R)
        klo = sb("k_lo", [P, 2, 2, T], F32R)
        vt = sb("v_channels", [P, T])
        vst = sb("v_pixels", [P, NC8, 4, D], F32R)
        probs = [sb(f"probs{i}", [P, T]) for i in range(4)]
        pt = [sb(f"probs_t{n}", [P, 2, NC8, 256], F32R) for n in ("hi", "lo")]
        o_half = sb("o_half", [P, 256])
        o_sum = sb("o_sum", [P, BANK])
        o_hi = sb("o_hi", [P, BANK], F32R)
        o_lo = sb("o_lo", [P, BANK], F32R)
        ident = sb("ident", [P, P])
        averager = sb("averager", [P, P])
        bias = sb("bias", [P, LAYERS * PAIRS, 3])
        gnw = sb("gnw", [P, LAYERS, KC])
        gnb = sb("gnb", [P, LAYERS, KC])
        gate = sb("gate", [P, LAYERS, 2])
        oscale = sb("oscale", [P, LAYERS])
        obias = sb("obias", [P, LAYERS, KC])
        zero = sb("zero", [P, 1])
        stats = sb("stats", [P, KC, 2, 6])
        moments = sb("moments", [P, KC, 2])
        gmean = sb("gmean", [P, KC])
        cvar = sb("cvar", [P, KC])
        rstd = sb("rstd", [P, KC])
        power = sb("power", [P, KC])
        coef_a0 = sb("coef_a0", [P, KC])
        coef_a = sb("coef_a", [P, KC])
        coef_b = sb("coef_b", [P, KC])
        neg_max = sb("neg_max", [P, 2])
        row_sum = sb("row_sum", [P, 2])
        row_inv = sb("row_inv", [P, 4])

        ps_s = [ctx.enter_context(nc.psum_tensor(f"ps_scores{i}", [P, T], F32)) for i in range(2)]
        ps_t = ctx.enter_context(nc.psum_tensor("ps_transposed", [P, T], F32))
        ps_m = [ctx.enter_context(nc.psum_tensor(f"ps_small{i}", [P, BANK], F32)) for i in range(2)]

        scores_ready = sem("scores_ready")
        scores_free = sem("scores_free")
        max_ready = sem("max_ready")
        exp_done = sem("exp_done")
        inv_ready = sem("inv_ready")
        probs_ready = sem("probs_ready")
        t_ready = sem("t_ready")
        t_hi = sem("t_hi")
        t_lo = sem("t_lo")
        small_free = [sem(f"small_free{i}") for i in range(2)]
        to_act = sem("to_act")
        to_dve = sem("to_dve")
        hi_out = sem("hi_out")
        q_out = sem("q_out")
        k_out = sem("k_out")
        q_stacked = sem("q_stacked")
        k_stacked = sem("k_stacked")
        w_used = sem("w_used")
        w_ready = [sem(f"w_ready_{n}") for n in "qkv"]
        wp_used = sem("wp_used")
        wp_ready = sem("wp_ready")
        o_out = sem("o_out")
        o_split = sem("o_split")
        o_hi_done = sem("o_hi_done")
        acc_ready = sem("acc_ready")
        acc_done = sem("acc_done")
        out_ready = sem("out_ready")
        stored = sem("stored")
        copied = sem("copied")
        raw_ready = sem("raw_ready")
        raw_used = sem("raw_used")
        dve_own = sem("dve_own")
        moments_ready = sem("moments_ready")
        var_ready = sem("var_ready")
        rstd_ready = sem("rstd_ready")
        coef_ready = sem("coef_ready")
        xn_ready = sem("xn_ready")
        x_hi = sem("x_hi")
        x_split = sem("x_split")
        params = sem("params")
        const_ready = sem("const_ready")
        pool_own = sem("pool_own")
        w_raw = [sem(f"w_raw{i}") for i in range(2)]
        w_hi = sem("w_hi")
        w_lo = sem("w_lo")
        w_stored = sem("w_stored")

        bank = group_banks()
        w_slots = [probs[0], probs[1], probs[2], probs[3]]
        LP = LAYERS * PAIRS

        def pt_flat(part, s):
            return pt[part][:, s].rearrange("p c q -> p (c q)")

        block = ctx.enter_context(nc.Block())

        @block.sync
        def _(sp):
            sp.dma_start(bias[:], b.rearrange("t p j -> p t j")).then_inc(params, 16)
            sp.dma_start(gnw[:, 0, :], gn[0]).then_inc(params, 16)
            sp.dma_start(gnb[:, 0, :], gn[1]).then_inc(params, 16)
            sp.dma_start(obias[:], pb.rearrange("l p c -> p l c")).then_inc(params, 16)
            for t in range(2):
                for h in range(2):
                    sp.dma_start(probs[2 * t + h][:], w[t, :, 2 * h:2 * h + 2, :].rearrange("p s n -> p (s n)")).then_inc(w_raw[t], 16)
            sp.dma_start(raw[:], x[0].rearrange("(c p) t -> p c t", p=P)).then_inc(raw_ready, 16)
            for t in range(LP):
                s = t % 2
                sp.wait_ge(w_lo, 1).then_inc(w_lo, -1)
                for part in (HI, LO):
                    sp.dma_start(split_w[t, :, :, part, :], pt_flat(part, s).bitcast(F32).rearrange("p (s n) -> p s n", s=4)).then_inc(w_stored, 16)
                if t + 2 < LP:
                    for h in range(2):
                        sp.dma_start(probs[2 * s + h][:], w[t + 2, :, 2 * h:2 * h + 2, :].rearrange("p s n -> p (s n)")).then_inc(w_raw[s], 16)
                sp.wait_ge(w_stored, 32 * (t + 1))
                if t == 0:
                    for j in range(3):
                        sp.dma_start(wt[j][:].bitcast(F32), split_w[0, :, j].rearrange("p a (k m) -> p a k m", k=KC)).then_inc(w_ready[j], 16)
                    sp.dma_start(wp[:].bitcast(F32), split_w[0, :, 3].rearrange("p a (k m) -> p a k m", k=KC)).then_inc(wp_ready, 16)
            sp.dma_start(y[0:IMAGES].rearrange("i (a c) t -> (i a) (c t)", a=16), x.rearrange("i (a c) t -> (i a) (c t)", a=16)).then_inc(copied, 16)

            def stack_q(par):
                sp.wait_ge(q_out, 1).then_inc(q_out, -1)
                for h in range(2):
                    for part in (HI, LO):
                        sp.dma_start(qst[part * D:part * D + D, par, h, :].bitcast(F32), nat[h * D:h * D + D, part, :].bitcast(F32)).then_inc(q_stacked, 16)

            def stack_k(par):
                sp.wait_ge(k_out, 1).then_inc(k_out, -1)
                for h in range(2):
                    for dst, part in ((khi, HI), (klo, LO)):
                        for up in range(2):
                            sp.dma_start(dst[up * D:up * D + D, par, h, :].bitcast(F32), nat[h * D:h * D + D, part, :].bitcast(F32)).then_inc(k_stacked, 16)

            def load_w(j, t):
                sp.wait_ge(w_used, 1).then_inc(w_used, -1)
                sp.dma_start(wt[j][:].bitcast(F32), split_w[bass.ds(t, 1), :, j].rearrange("o p a (k m) -> (o p) a k m", k=KC)).then_inc(w_ready[j], 16)

            stack_q(0)
            load_w(0, 1)
            stack_k(0)
            load_w(1, 1)
            load_w(2, 1)
            def store_image(at):
                for c in range(KC):
                    sp.wait_ge(out_ready, 1).then_inc(out_ready, -1)
                    sp.dma_start(y[bass.ds(at, 1), c * P:(c + 1) * P, :].rearrange("o p t -> (o p) t"), acc[:, c, :]).then_inc(stored, 16)
                sp.wait_ge(stored, KC * 16).then_inc(stored, -KC * 16)

            with sp.Fori(0, TURNS) as i:
                layer = i // IMAGES
                layer_next = (i + 1) // IMAGES % LAYERS
                for p in range(PAIRS):
                    sp.wait_ge(wp_used, 1).then_inc(wp_used, -1)
                    sp.dma_start(wp[:].bitcast(F32), split_w[bass.ds(layer * PAIRS + p, 1), :, 3].rearrange("o p a (k m) -> (o p) a k m", k=KC)).then_inc(wp_ready, 16)
                    if p == 0:
                        store_image(i + IMAGES)
                        sp.wait_ge(copied, 16)
                        sp.dma_start(acc[:], y[bass.ds(i + layer, 1)].rearrange("o (c p) t -> p (o c) t", p=P)).then_inc(acc_ready, 16)
                    if p == 1:
                        sp.wait_ge(raw_used, KC).then_inc(raw_used, -KC)
                        sp.dma_start(raw[:], y[bass.ds(i + 1 + (i + 1) // IMAGES, 1)].rearrange("o (c p) t -> p (o c) t", p=P)).then_inc(raw_ready, 16)
                    after = layer * PAIRS + p + 2 if p < 2 else layer_next * PAIRS + p - 2
                    stack_q((p + 1) % 2)
                    load_w(0, after)
                    stack_k((p + 1) % 2)
                    load_w(1, after)
                    load_w(2, after)
            store_image(TURNS + IMAGES)
            for j in range(3):
                sp.wait_ge(w_ready[j], 16)

        @block.tensor
        def _(pe):
            def start_small(key):
                n = bank[key]
                pe.wait_ge(small_free[n], 1).then_inc(small_free[n], -1)
                return ps_m[n]

            def project_in(j, key, half):
                if half == 0:
                    pe.wait_ge(w_ready[j], 16).then_inc(w_ready[j], -16)
                out = start_small(key)
                cols = slice(half * HALF, (half + 1) * HALF)
                terms = [(wl, xl, k) for k in range(KC) for wl, xl in ((HI, HI), (HI, LO), (LO, HI))]
                for n, (wl, xl, k) in enumerate(terms):
                    last = nc.tensor.matmul(out[:], wt[j][:, wl, k, :], xs[:, xl, k, cols], start=n == 0, stop=n == len(terms) - 1)
                last.then_inc(to_act, 1)

            def scores(u, par):
                pe.wait_ge(scores_free, 1).then_inc(scores_free, -1)
                h, qb = head_of(u), u // 2
                for half in range(2):
                    cols = slice(half * HALF, (half + 1) * HALF)
                    for n, k in enumerate((khi, klo)):
                        last = nc.tensor.matmul(ps_s[u % 2][:, cols], qst[:, par, h, qb * P:(qb + 1) * P], k[:, par, h, cols], start=n == 0, stop=n == 1)
                last.then_inc(scores_ready, 1)

            def transposes(u):
                pe.wait_ge(probs_ready, 1).then_inc(probs_ready, -1)
                for c in range(NC8):
                    last = nc.tensor.transpose(ps_t[:, c * P:(c + 1) * P], probs[u % 4][:, c * P:(c + 1) * P], ident[:])
                last.then_inc(t_ready, 1)

            def attend(key, h):
                out = start_small(key)
                for c in range(NC8):
                    for part in (HI, LO):
                        last = nc.tensor.matmul(out[:, 0:256], vst[:, c, 2 * h:2 * h + 2, :].rearrange("p a d -> p (a d)"), pt[part][:, h, c, :],
                                                start=c == 0 and part == HI, stop=c == NC8 - 1 and part == LO)
                last.then_inc(to_act, 1)

            def turn_v(key, half):
                out = start_small(key)
                for c in range(4):
                    last = nc.tensor.transpose(out[:, c * P:(c + 1) * P], vt[:, (4 * half + c) * P:(4 * half + c + 1) * P], ident[:])
                last.then_inc(to_act, 1)

            def project_out(key, c):
                out = start_small(key)
                for n, (wl, o) in enumerate(((HI, o_hi), (HI, o_lo), (LO, o_hi))):
                    last = nc.tensor.matmul(out[:], wp[:, wl, c, :], o[:], start=n == 0, stop=n == 2)
                last.then_inc(to_dve, 1)

            def group_mean(key):
                pe.wait_ge(moments_ready, 1).then_inc(moments_ready, -1)
                out = start_small(key)
                nc.tensor.matmul(out[:, 0:2 * KC], averager[:], moments[:].rearrange("p c s -> p (c s)"), start=True, stop=True).then_inc(to_dve, 1)

            def group_var(key):
                pe.wait_ge(moments_ready, 1).then_inc(moments_ready, -1)
                out = start_small(key)
                nc.tensor.matmul(out[:, 0:KC], averager[:], cvar[:], start=True, stop=True).then_inc(to_dve, 1)

            def both_banks_read():
                pe.wait_ge(small_free[0], 1)
                pe.wait_ge(small_free[1], 1)

            def run(key):
                kind = key[1]
                if kind == "pv":
                    attend(key, key[2])
                elif kind == "vt":
                    turn_v(key, key[2])
                elif kind == "proj":
                    if key[2:] == (0, 0):
                        pe.wait_ge(wp_ready, 16).then_inc(wp_ready, -16)
                    if key[3] == 0:
                        pe.wait_ge(o_split, 1).then_inc(o_split, -1)
                    project_out(key, key[3])
                elif kind in "qkv":
                    project_in("qkv".index(kind), key, key[2])
                elif kind == "mean":
                    group_mean(key)
                elif kind == "var":
                    group_var(key)

            pe.wait_ge(const_ready, 2)
            group_mean((NORM_PAIR, "mean"))
            group_var((NORM_PAIR, "var"))
            pe.wait_ge(x_split, KC).then_inc(x_split, -KC)
            for kind, out in (("q", q_out), ("k", k_out), ("v", None)):
                for half in range(2):
                    run((3, kind, half))
                if out is not None:
                    both_banks_read()
                    pe.sem_inc(out, 1)
            pe.wait_ge(wp_ready, 16).then_inc(wp_ready, -16)
            pe.wait_ge(k_stacked, 128).then_inc(k_stacked, -128)
            for u in range(3):
                scores(u, 0)

            with pe.Fori(0, TURNS):
                for p in range(PAIRS):
                    par = p % 2
                    for u, items in enumerate(schedule(p)):
                        pe.wait_ge(t_lo, 1).then_inc(t_lo, -1)
                        transposes(u)
                        if u + 3 == SLOTS:
                            pe.wait_ge(k_stacked, 128).then_inc(k_stacked, -128)
                        scores((u + 3) % SLOTS, par if u + 3 < SLOTS else 1 - par)
                        if u == q_out_slot(p):
                            both_banks_read()
                            pe.sem_inc(q_out, 1)
                        if u == K_OUT_SLOT:
                            both_banks_read()
                            pe.sem_inc(k_out, 1)
                        if u in O_OUT_SLOTS.values():
                            both_banks_read()
                            pe.sem_inc(o_out, 1)
                        if p == 0 and u == 3:
                            both_banks_read()
                            pe.sem_inc(acc_done, 1)
                        if p == PAIRS - 1 and u == 5:
                            pe.wait_ge(x_split, KC).then_inc(x_split, -KC)
                        for item in items:
                            run((p, *item))
            pe.wait_ge(t_lo, 1).then_inc(t_lo, -1)
            run((0, "pv", 1, 3))
            both_banks_read()
            pe.sem_inc(o_out, 1)
            for c in range(KC):
                run((0, "proj", 1, c))
            both_banks_read()
            pe.sem_inc(acc_done, 1)

        @block.scalar
        def _(act):
            def exps(u):
                act.wait_ge(max_ready, 1).then_inc(max_ready, -1)
                nc.scalar.activation(probs[u % 4][:], ps_s[u % 2][:], ACT.Exp, bias=neg_max[:, u % 2:u % 2 + 1],
                                     accum_out=row_sum[:, u % 2:u % 2 + 1]).then_inc(exp_done, 1)

            def round_qk(p, name, half, bias_ap):
                act.wait_ge(to_act, 1).then_inc(to_act, -1)
                nc.scalar.activation(nat[:, HI, half * HALF:(half + 1) * HALF], ps_m[bank[(p, name, half)]][:], ACT.Identity, bias=bias_ap).then_inc(hi_out, 1)
                if half == 1:
                    act.sem_inc(w_used, 1)

            def round_v(p, half):
                act.wait_ge(to_act, 1).then_inc(to_act, -1)
                nc.scalar.activation(vst[:, 4 * half:4 * half + 4, 0:4:3, :], ps_m[bank[(p, "vt", half)]][:].rearrange("p (c h d) -> p c h d", c=4, h=2), ACT.Copy).then_inc(hi_out, 1)

            def finish(c, at):
                nc.scalar.activation(acc[:, c, :], acc[:, c, :], ACT.Identity, bias=obias[:, bass.ds(at, 1), c:c + 1].rearrange("p o c -> p (o c)"),
                                     scale=oscale[:, bass.ds(at, 1)]).then_inc(out_ready, 1)

            def run(p, kind, where, bias_of):
                if kind == "pv":
                    far_half(p, *where)
                elif kind == "vt":
                    round_v(p, where[0])
                elif kind in ("q", "k"):
                    if (kind, *where) == ("k", 0):
                        act.wait_ge(q_stacked, 64).then_inc(q_stacked, -64)
                    round_qk(p, kind, where[0], bias_of("qk".index(kind)))
                elif kind == "v":
                    add_bias_v(p, where[0], bias_of(2))

            def add_bias_v(p, half, bias_ap):
                act.wait_ge(to_act, 1).then_inc(to_act, -1)
                n = bank[(p, "v", half)]
                nc.scalar.activation(vt[:, half * HALF:(half + 1) * HALF], ps_m[n][:], ACT.Identity, bias=bias_ap).then_inc(small_free[n], 1)
                if half == 1:
                    act.sem_inc(w_used, 1)

            def far_half(p, h, qt):
                act.wait_ge(to_act, 1).then_inc(to_act, -1)
                nc.scalar.activation(o_half[h * D:(h + 1) * D, :], ps_m[bank[(p, "pv", h, qt)]][(1 - h) * D:(2 - h) * D, 0:256], ACT.Copy).then_inc(hi_out, 1)

            def normalise(c):
                nc.scalar.activation(raw[:, c, :], raw[:, c, :], ACT.Identity, bias=coef_b[:, c:c + 1], scale=coef_a[:, c:c + 1]).then_inc(xn_ready, 1)

            for t in range(LP):
                act.wait_ge(w_raw[t % 2], 32 * (t // 2 + 1))
                if t >= 2:
                    act.wait_ge(w_stored, 32 * (t - 1))
                flat = pt_flat(HI, t % 2)
                nc.scalar.activation(flat[:, 0:512], probs[2 * (t % 2)][:, 0:512], ACT.Copy, scale=SCALE)
                nc.scalar.activation(flat[:, 512:1024], probs[2 * (t % 2)][:, 512:1024], ACT.Copy)
                nc.scalar.activation(flat[:, 1024:2048], probs[2 * (t % 2) + 1][:], ACT.Copy).then_inc(w_hi, 1)
            act.wait_ge(coef_ready, 1).then_inc(coef_ready, -1)
            for c in range(KC):
                normalise(c)
            for kind in "qkv":
                for half in range(2):
                    run(3, kind, (half,), lambda j: bias[:, 0, j:j + 1])
            act.wait_ge(w_stored, 32 * LP)
            exps(0)
            exps(1)

            with act.Fori(0, TURNS) as i:
                layer = i // IMAGES
                layer_next = (i + 1) // IMAGES % LAYERS
                layer_last = (i + TURNS - 1) // IMAGES % LAYERS
                for p in range(PAIRS):
                    pair = layer * PAIRS + p + 1 if p < 3 else layer_next * PAIRS

                    def bias_of(j):
                        return bias[:, bass.ds(pair, 1), j:j + 1].rearrange("p o j -> p (o j)")

                    for u, items in enumerate(schedule(p)):
                        h, qb = head_of(u), u // 2
                        act.wait_ge(t_ready, 1).then_inc(t_ready, -1)
                        nc.scalar.activation(pt[HI][:, h, :, (qb % 2) * P:(qb % 2 + 1) * P], ps_t[:].rearrange("p (c q) -> p c q", q=P), ACT.Copy).then_inc(t_hi, 1)
                        exps((u + 2) % SLOTS)
                        for kind, *where in items:
                            run(p, kind, where, bias_of)
                        if p == 0 and 3 <= u < 3 + KC:
                            if u == 3:
                                act.wait_ge(acc_done, 1).then_inc(acc_done, -1)
                            finish(u - 3, layer_last)
                        if p == NORM_PAIR and u >= 14:
                            if u == 14:
                                act.wait_ge(coef_ready, 1).then_inc(coef_ready, -1)
                            normalise(2 * (u - 14))
                            normalise(2 * (u - 14) + 1)
            far_half(0, 1, 3)
            act.wait_ge(acc_done, 1).then_inc(acc_done, -1)
            for c in range(KC):
                finish(c, LAYERS - 1)

        @block.vector
        def _(dve):
            def own(instruction):
                instruction.then_inc(dve_own, 1)
                dve.wait_ge(dve_own, 1).then_inc(dve_own, -1)

            def maxima(u):
                dve.wait_ge(scores_ready, 1).then_inc(scores_ready, -1)
                nc.vector.tensor_reduce(neg_max[:, u % 2:u % 2 + 1], ps_s[u % 2][:], AX_X, ALU.max, negate=True).then_inc(max_ready, 1)

            def inverse(u):
                dve.wait_ge(exp_done, 1).then_inc(exp_done, -1)
                dve.sem_inc(scores_free, 1)
                nc.vector.reciprocal(row_inv[:, u % 4:u % 4 + 1], row_sum[:, u % 2:u % 2 + 1]).then_inc(inv_ready, 1)

            def rest_qk(p, name, half, bias_ap):
                dve.wait_ge(hi_out, 1).then_inc(hi_out, -1)
                n = bank[(p, name, half)]
                cols = slice(half * HALF, (half + 1) * HALF)
                nc.vector.scalar_tensor_tensor(out=nat[:, LO, cols], in0=ps_m[n][:], scalar=bias_ap, in1=nat[:, HI, cols].bitcast(F32),
                                               op0=ALU.add, op1=ALU.subtract).then_inc(small_free[n], 1)

            def sum_halves(p, h, qt):
                dve.wait_ge(hi_out, 1).then_inc(hi_out, -1)
                n = bank[(p, "pv", h, qt)]
                rows = slice(h * D, (h + 1) * D)
                nc.vector.tensor_tensor(o_sum[rows, (qt % 2) * 256:(qt % 2 + 1) * 256], ps_m[n][rows, 0:256], o_half[rows, :], ALU.add).then_inc(small_free[n], 1)

            def add_projection(p, half, c):
                dve.wait_ge(to_dve, 1).then_inc(to_dve, -1)
                n = bank[(p, "proj", half, c)]
                cols = slice(half * HALF, (half + 1) * HALF)
                nc.vector.tensor_tensor(acc[:, c, cols], ps_m[n][:], acc[:, c, cols], ALU.add).then_inc(small_free[n], 1)

            def channel_stats(n):
                c, half = n // 2, n % 2
                if n == 0:
                    dve.wait_ge(raw_ready, 16).then_inc(raw_ready, -16)
                own(nc.vector.bn_stats(stats[:, c, half, :], raw[:, c, half * HALF:(half + 1) * HALF]))

            def channel_moments():
                for c in range(KC):
                    last = nc.vector.bn_aggr(moments[:, c, :], stats[:, c])
                last.then_inc(moments_ready, 1)

            def group_means():
                dve.wait_ge(to_dve, 1).then_inc(to_dve, -1)
                n = bank[(NORM_PAIR, "mean")]
                own(nc.vector.tensor_copy(gmean[:], ps_m[n][:, 0:2 * KC].rearrange("p (c s) -> p c s", s=2)[:, :, 0]))
                dve.sem_inc(small_free[n], 1)
                own(nc.vector.tensor_tensor(cvar[:], moments[:, :, 0], gmean[:], ALU.subtract))
                own(nc.vector.tensor_tensor(cvar[:], cvar[:], cvar[:], ALU.mult))
                nc.vector.tensor_tensor(cvar[:], cvar[:], moments[:, :, 1], ALU.add).then_inc(moments_ready, 1)

            def group_vars():
                dve.wait_ge(to_dve, 1).then_inc(to_dve, -1)
                n = bank[(NORM_PAIR, "var")]
                own(nc.vector.tensor_scalar(rstd[:], ps_m[n][:, 0:KC], EPS, None, ALU.add))
                dve.sem_inc(small_free[n], 1)
                dve.sem_inc(var_ready, 1)

            def coefficients(at):
                dve.wait_ge(rstd_ready, 1).then_inc(rstd_ready, -1)
                w_ap = gnw[:, bass.ds(at, 1), :].rearrange("p o c -> p (o c)")
                b_ap = gnb[:, bass.ds(at, 1), :].rearrange("p o c -> p (o c)")
                on = gate[:, bass.ds(at, 1), 0:1].rearrange("p o c -> p (o c)")
                off = gate[:, bass.ds(at, 1), 1:2].rearrange("p o c -> p (o c)")
                own(nc.vector.tensor_tensor(coef_a0[:], rstd[:], w_ap, ALU.mult))
                own(nc.vector.tensor_tensor(coef_b[:], gmean[:], coef_a0[:], ALU.mult))
                own(nc.vector.tensor_tensor(coef_b[:], b_ap, coef_b[:], ALU.subtract))
                own(nc.vector.tensor_scalar(coef_b[:], coef_b[:], on, None, ALU.mult))
                nc.vector.tensor_scalar(coef_a[:], coef_a0[:], on, off, ALU.mult, ALU.add).then_inc(coef_ready, 1)

            def round_x(c):
                dve.wait_ge(xn_ready, 1).then_inc(xn_ready, -1)
                nc.vector.tensor_copy(xs[:, HI, c, :], raw[:, c, :]).then_inc(x_hi, 1)

            def rest_v(p, half):
                dve.wait_ge(hi_out, 1).then_inc(hi_out, -1)
                n = bank[(p, "vt", half)]
                nc.vector.tensor_tensor(vst[:, 4 * half:4 * half + 4, 1:3, :], ps_m[n][:].rearrange("p (c h d) -> p c h d", c=4, h=2),
                                        vst[:, 4 * half:4 * half + 4, 0:4:3, :].bitcast(F32), ALU.subtract).then_inc(small_free[n], 1)

            def run(p, kind, where, bias_of):
                if kind == "pv":
                    sum_halves(p, *where)
                elif kind == "vt":
                    rest_v(p, where[0])
                elif kind in ("q", "k"):
                    rest_qk(p, kind, where[0], bias_of("qk".index(kind)))
                elif kind == "proj":
                    if p == 0 and tuple(where) == (0, 0):
                        dve.wait_ge(acc_ready, 16).then_inc(acc_ready, -16)
                    add_projection(p, *where)
                    if tuple(where) == (1, KC - 1):
                        dve.sem_inc(wp_used, 1)
                elif kind == "mean":
                    group_means()
                elif kind == "var":
                    group_vars()

            nc.vector.memset(vst[:].rearrange("p c a d -> p (c a d)").bitcast(F32), 0.0)
            nc.vector.memset(acc[:].rearrange("p c t -> p (c t)"), 0.0)
            nc.vector.memset(o_sum[:], 0.0)
            nc.vector.memset(gate[:, 0, 0:1], 1.0)
            nc.vector.memset(gate[:, 0, 1:2], 0.0)
            nc.vector.memset(gate[:, 1, 0:1], 0.0)
            nc.vector.memset(gate[:, 1, 1:2], 1.0)
            nc.vector.memset(gnw[:, 1, :], 0.0)
            nc.vector.memset(gnb[:, 1, :], 0.0)
            nc.vector.memset(oscale[:, 0:1], 2.0 ** -0.5)
            own(nc.vector.memset(oscale[:, 1:2], 1.0))
            dve.wait_ge(params, 64)
            own(nc.vector.tensor_scalar(bias[:, :, 0], bias[:, :, 0], SCALE, None, ALU.mult))
            own(nc.vector.tensor_scalar(obias[:, 0, :], obias[:, 0, :], oscale[:, 0:1], None, ALU.mult))
            for n in range(2):
                dve.sem_inc(small_free[n], 1)
            dve.sem_inc(scores_free, 2)
            dve.sem_inc(t_lo, 1)
            for t in range(LP):
                dve.wait_ge(w_hi, 1).then_inc(w_hi, -1)
                hi, lo = pt_flat(HI, t % 2).bitcast(F32), pt_flat(LO, t % 2)
                if t >= 2:
                    dve.wait_ge(w_stored, 32 * (t - 1))
                nc.vector.scalar_tensor_tensor(out=lo[:, 0:512], in0=probs[2 * (t % 2)][:, 0:512], scalar=SCALE, in1=hi[:, 0:512], op0=ALU.mult, op1=ALU.subtract)
                nc.vector.tensor_tensor(lo[:, 512:1024], probs[2 * (t % 2)][:, 512:1024], hi[:, 512:1024], ALU.subtract)
                nc.vector.tensor_tensor(lo[:, 1024:2048], probs[2 * (t % 2) + 1][:], hi[:, 1024:2048], ALU.subtract).then_inc(w_lo, 1)
            for n in range(2 * KC):
                channel_stats(n)
            channel_moments()
            group_means()
            group_vars()
            coefficients(0)
            for c in range(KC):
                round_x(c)
            for kind in "qk":
                for half in range(2):
                    run(3, kind, (half,), lambda j: bias[:, 0, j:j + 1])
            dve.wait_ge(w_stored, 32 * LP)
            maxima(0)
            maxima(1)
            inverse(0)

            with dve.Fori(0, TURNS) as i:
                layer = i // IMAGES
                layer_next = (i + 1) // IMAGES % LAYERS
                for p in range(PAIRS):
                    pair = layer * PAIRS + p + 1 if p < 3 else layer_next * PAIRS

                    def bias_of(j):
                        return bias[:, bass.ds(pair, 1), j:j + 1].rearrange("p o j -> p (o j)")

                    for u, items in enumerate(schedule(p)):
                        h, qb = head_of(u), u // 2
                        inverse((u + 1) % SLOTS)
                        maxima((u + 2) % SLOTS)
                        dve.wait_ge(t_hi, 1).then_inc(t_hi, -1)
                        cols = slice((qb % 2) * P, (qb % 2 + 1) * P)
                        nc.vector.tensor_tensor(pt[LO][:, h, :, cols], ps_t[:].rearrange("p (c q) -> p c q", q=P), pt[HI][:, h, :, cols].bitcast(F32), ALU.subtract).then_inc(t_lo, 1)
                        for kind, *where in items:
                            run(p, kind, where, bias_of)
                        if p == NORM_PAIR:
                            if u < 8:
                                channel_stats(u)
                            if u == 8:
                                channel_moments()
                            if u == 13:
                                coefficients(layer_next)
                        if p == PAIRS - 1 and u < KC:
                            round_x(u)
            sum_halves(0, 1, 3)
            for c in range(KC):
                add_projection(0, 1, c)

        @block.gpsimd
        def _(pool):
            def own(instruction):
                instruction.then_inc(pool_own, 1)
                pool.wait_ge(pool_own, 1).then_inc(pool_own, -1)

            def scale_probs(u):
                pool.wait_ge(inv_ready, 1).then_inc(inv_ready, -1)
                nc.gpsimd.tensor_tensor(probs[u % 4][:], probs[u % 4][:], row_inv[:, u % 4:u % 4 + 1].to_broadcast([P, T]), ALU.mult).then_inc(probs_ready, 1)

            def split_o():
                pool.wait_ge(o_out, 1).then_inc(o_out, -1)
                own(nc.gpsimd.tensor_tensor(o_hi[:], o_sum[:], zero[:, 0:1].to_broadcast([P, BANK]), ALU.add))
                nc.gpsimd.tensor_tensor(o_lo[:], o_sum[:], o_hi[:].bitcast(F32), ALU.subtract).then_inc(o_split, 1)

            def rest_x(c):
                pool.wait_ge(x_hi, 1).then_inc(x_hi, -1)
                own(nc.gpsimd.tensor_tensor(xs[:, LO, c, :], raw[:, c, :], xs[:, HI, c, :].bitcast(F32), ALU.subtract))
                pool.sem_inc(x_split, 1)
                pool.sem_inc(raw_used, 1)

            def inverse_root():
                pool.wait_ge(var_ready, 1).then_inc(var_ready, -1)
                nc.gpsimd.tensor_tensor(rstd[:], rstd[:], power[:], ALU.pow).then_inc(rstd_ready, 1)

            own(nc.gpsimd.memset(ident[:], 0.0))
            nc.gpsimd.affine_select(out=ident[:], in_=ident[:], compare_op=ALU.not_equal, fill=1.0, base=0,
                                    pattern=[[-1, P]], channel_multiplier=1).then_inc(const_ready, 1)
            per_group = C // GROUPS
            own(nc.gpsimd.memset(averager[:], 1.0 / per_group))
            by_group = averager[:].rearrange("p (g m) -> p g m", m=per_group)
            own(nc.gpsimd.affine_select(out=by_group, in_=by_group, compare_op=ALU.is_ge, fill=0.0, base=0,
                                        pattern=[[-per_group, P // per_group], [0, per_group]], channel_multiplier=1))
            nc.gpsimd.affine_select(out=by_group, in_=by_group, compare_op=ALU.is_ge, fill=0.0, base=per_group - 1,
                                    pattern=[[per_group, P // per_group], [0, per_group]], channel_multiplier=-1).then_inc(const_ready, 1)
            nc.gpsimd.memset(zero[:], 0.0)
            own(nc.gpsimd.memset(power[:], -0.5))
            inverse_root()
            for c in range(KC):
                rest_x(c)
            scale_probs(0)
            with pool.Fori(0, TURNS):
                for p in range(PAIRS):
                    for u in range(SLOTS):
                        scale_probs((u + 1) % SLOTS)
                        if u in O_OUT_SLOTS.values():
                            split_o()
                        if p == NORM_PAIR and u == 12:
                            inverse_root()
                        if p == PAIRS - 1 and u < KC:
                            rest_x(u)
            split_o()


def kernel(x, L0_conv_gn_w, L0_conv_gn_b, L0_conv_qkv_w, L0_conv_qkv_b, L0_conv_proj_w, L0_conv_proj_b,
           L1_conv_w_qkv, L1_conv_b_qkv, L1_conv_w_proj, L1_conv_b_proj):
    import numpy as np
    import concourse.bacc as bacc
    from concourse.bass_utils import run_bass_kernel_spmd

    B, C, H, W = x.shape
    pairs, d = HEADS // 2, C // HEADS

    def lay_in(w_in, w_out):
        q = np.asarray(w_in).reshape(C // P, P, pairs, 2, 3, d).transpose(2, 1, 4, 0, 3, 5).reshape(pairs, P, 3, C)
        o = np.asarray(w_out).reshape(pairs, P, 1, C)
        return np.concatenate([q, o], 2)

    def lay_bias(v):
        return np.asarray(v).reshape(pairs, 2, 3, d).transpose(0, 1, 3, 2).reshape(pairs, P, 3)

    def lay_channels(v):
        return np.asarray(v).reshape(C // P, P).T

    arrays = {
        "x": np.asarray(x).reshape(B, C, H * W),
        "w": np.concatenate([lay_in(np.asarray(L0_conv_qkv_w).T, np.asarray(L0_conv_proj_w).T), lay_in(L1_conv_w_qkv, L1_conv_w_proj)]),
        "b": np.concatenate([lay_bias(L0_conv_qkv_b), lay_bias(L1_conv_b_qkv)]),
        "gn": np.stack([lay_channels(L0_conv_gn_w), lay_channels(L0_conv_gn_b)]),
        "pb": np.stack([lay_channels(L0_conv_proj_b), lay_channels(L1_conv_b_proj)]),
    }
    arrays = {k: np.ascontiguousarray(a) for k, a in arrays.items()}
    nc = bacc.Bacc("TRN2", target_bir_lowering=False, num_devices=1)
    aps = [nc.dram_tensor(n, a.shape, mybir.dt.from_np(a.dtype), kind="ExternalInput").ap() for n, a in arrays.items()]
    y = nc.dram_tensor("y", (3 * B + 1, C, H * W), F32, kind="ExternalOutput").ap()
    build(nc, *aps, y)
    r = run_bass_kernel_spmd(nc, [arrays], core_ids=[0])
    return r.results[0]["y"][2 * B + 1:].reshape(B, C, H, W)
```

```python
from contextlib import ExitStack

import concourse.bass as bass
from concourse import mybir

F32 = mybir.dt.float32
F32R = mybir.dt.float32r
ALU = mybir.AluOpType
ACT = mybir.ActivationFunctionType
AX_X = mybir.AxisListType.X

P = 128
LAYERS = 2
HEADS = 8
BANK = 512
GROUPS = 32
EPS = 1e-6
HI, LO = 0, 1
SLOTS = 16

STATS_SLOTS = [(0, 5), (0, 7), (0, 8), (0, 9), (0, 14), (0, 15), (1, 4), (1, 5)]
STATS_PAIR = 1
MOMENTS_SLOT = 5
MEAN_SLOT, VAR_SLOT = 7, 14
NORM_PAIR = 2
NORM_SLOT = 6
X_SLOTS = [(2, 10, 0, 0), (2, 11, 0, 1), (2, 13, 0, 2), (2, 15, 0, 3),
           (3, 0, 1, 0), (3, 3, 1, 1), (3, 4, 1, 2), (3, 4, 1, 3)]
Q_OUT_SLOTS = (3, 7)
K_OUT_SLOTS = (10, 11)
O_OUT_SLOTS = (1, 9)
ACC_OUT_SLOT = 4
SPLIT_W = {"v": (3, 4), "o": (7, 8), "q": (10, 11), "k": (14, 15)}


def head_of(u):
    return u % 2


def schedule(p):
    between, after = [None] * SLOTS, [None] * SLOTS
    for u in range(SLOTS):
        if u % 4 == 3:
            between[u] = ("pv", 0, u // 4)
        if u % 4 == 0:
            between[u] = ("pv", 1, (u // 4 - 1) % 4)
    after[0], between[1] = ("vt", 0), ("vt", 1)
    for c in range(4):
        after[2 + c] = ("proj", 1, c)
        after[10 + c] = ("proj", 0, c)
    for u, item in {2: ("q", 0), 5: ("v", 0), 6: ("q", 1), 9: ("k", 0), 10: ("k", 1), 14: ("v", 1)}.items():
        between[u] = item
    if p == STATS_PAIR:
        after[MEAN_SLOT], after[VAR_SLOT] = ("mean",), ("var",)
    return between, after


def group_banks():
    order = [(p, *item) for p in range(4) for pair in zip(*schedule(p)) for item in pair if item]
    assert len(order) % 2 == 0
    return {key: n % 2 for n, key in enumerate(order)}


def build(nc, x, w, b, gn, pb, y):
    IMAGES, C, T = x.shape
    KC = C // P
    PAIRS = HEADS // 2
    D = C // HEADS
    SCALE = float(D) ** -0.5
    HALF = T // 2
    NC8 = T // P
    TURNS = LAYERS * IMAGES
    assert D == 64 and KC == 4 and PAIRS == 4 and HALF == BANK and NC8 * 2 == SLOTS

    with ExitStack() as ctx:
        def sb(name, shape, dt=F32):
            return ctx.enter_context(nc.sbuf_tensor(name, shape, dt))

        def sem(name):
            return ctx.enter_context(nc.semaphore(name))

        xs = sb("xs", [P, 2, KC, T], F32R)
        raw = sb("raw", [P, KC, T])
        acc = sb("acc", [P, KC, T])
        wt = {n: sb(f"w_{n}", [P, 2, KC, P], F32R) for n in "qkvo"}
        stage = sb("w_stage", [P, KC, P])
        nat = sb("nat", [P, 2, T], F32R)
        q_hl = sb("q_hi_lo", [P, 2, 2, T], F32R)
        q_lh = sb("q_lo_hi", [P, 2, 2, T], F32R)
        k_hl = sb("k_hi_lo", [P, 2, 2, T], F32R)
        vt = sb("v_channels", [P, T])
        vst = sb("v_pixels", [P, NC8, 4, D], F32R)
        probs = [sb(f"probs{i}", [P, T]) for i in range(4)]
        pt = [sb(f"probs_t{n}", [P, 2, NC8, 256], F32R) for n in ("hi", "lo")]
        o_half = sb("o_half", [P, 256])
        o_sum = sb("o_sum", [P, BANK])
        o_hi = sb("o_hi", [P, BANK], F32R)
        o_lo = sb("o_lo", [P, BANK], F32R)
        ident = sb("ident", [P, P])
        averager = sb("averager", [P, P])
        bias = sb("bias", [P, LAYERS * PAIRS, 3])
        gnw = sb("gnw", [P, LAYERS, KC])
        gnb = sb("gnb", [P, LAYERS, KC])
        gate = sb("gate", [P, LAYERS, 2])
        oscale = sb("oscale", [P, LAYERS])
        obias = sb("obias", [P, LAYERS, KC])
        stats = sb("stats", [P, KC, 2, 6])
        moments = sb("moments", [P, KC, 2])
        gmean = sb("gmean", [P, KC])
        cvar = sb("cvar", [P, KC])
        rstd = sb("rstd", [P, KC])
        power = sb("power", [P, KC])
        coef_a0 = sb("coef_a0", [P, KC])
        coef_a = sb("coef_a", [P, KC])
        coef_b = sb("coef_b", [P, KC])
        neg_max = sb("neg_max", [P, 2])
        row_sum = sb("row_sum", [P, 2])
        row_inv = sb("row_inv", [P, 4])

        ps_s = [ctx.enter_context(nc.psum_tensor(f"ps_scores{i}", [P, T], F32)) for i in range(2)]
        ps_t = ctx.enter_context(nc.psum_tensor("ps_transposed", [P, T], F32))
        ps_m = [ctx.enter_context(nc.psum_tensor(f"ps_small{i}", [P, BANK], F32)) for i in range(2)]

        scores_ready = sem("scores_ready")
        scores_free = sem("scores_free")
        max_ready = sem("max_ready")
        exp_done = sem("exp_done")
        inv_ready = sem("inv_ready")
        probs_ready = sem("probs_ready")
        t_ready = sem("t_ready")
        t_hi = sem("t_hi")
        t_lo = sem("t_lo")
        small_free = [sem(f"small_free{i}") for i in range(2)]
        to_act = sem("to_act")
        to_dve = sem("to_dve")
        hi_out = sem("hi_out")
        q_out = sem("q_out")
        k_out = sem("k_out")
        q_stacked = sem("q_stacked")
        k_stacked = sem("k_stacked")
        w_first = [sem(f"w_first{i}") for i in range(3)]
        stage_ready = sem("stage_ready")
        stage_used = sem("stage_used")
        wq_hi = sem("wq_hi")
        wq_lo = sem("wq_lo")
        w_hi = sem("w_hi")
        w_ready = {n: sem(f"w_ready_{n}") for n in "qkvo"}
        o_out = sem("o_out")
        o_hi_done = sem("o_hi_done")
        o_split = sem("o_split")
        acc_ready = [sem(f"acc_ready{c}") for c in range(KC)]
        acc_done = sem("acc_done")
        out_ready = sem("out_ready")
        stored = [sem(f"stored{c}") for c in range(KC)]
        raw_first = [sem(f"raw_first{c}") for c in range(KC)]
        raw_ready = sem("raw_ready")
        raw_used = sem("raw_used")
        dve_own = sem("dve_own")
        moments_ready = sem("moments_ready")
        var_ready = sem("var_ready")
        rstd_ready = sem("rstd_ready")
        coef_ready = sem("coef_ready")
        xn_ready = sem("xn_ready")
        x_hi = sem("x_hi")
        x_split = sem("x_split")
        params = sem("params")
        const_ready = sem("const_ready")
        pool_own = sem("pool_own")

        bank = group_banks()
        KINDS = "qkvo"
        Q_STACK = 8 * 16
        K_STACK = 4 * 16

        def first_w(t, kind):
            at = acc[:, 2, 0:BANK] if kind == "v" else acc[:, t, KINDS.index(kind) * BANK:(KINDS.index(kind) + 1) * BANK]
            return at.rearrange("p (k m) -> p k m", k=KC)

        block = ctx.enter_context(nc.Block())

        @block.sync
        def _(sp):
            for c in range(KC):
                sp.dma_start(raw[:, c, :], x[0, c * P:(c + 1) * P, :]).then_inc(raw_first[c], 16)
            sp.dma_start(acc[:, 0, :], w[0, :, 0:2, :].rearrange("p s n -> p (s n)")).then_inc(w_first[0], 16)
            sp.dma_start(acc[:, 2, 0:BANK], w[0, :, 2, :]).then_inc(w_first[1], 16)
            sp.dma_start(bias[:], b.rearrange("t p j -> p t j")).then_inc(params, 16)
            sp.dma_start(gnw[:, 0, :], gn[0]).then_inc(params, 16)
            sp.dma_start(gnb[:, 0, :], gn[1]).then_inc(params, 16)
            sp.dma_start(obias[:], pb.rearrange("l p c -> p l c")).then_inc(params, 16)
            sp.dma_start(acc[:, 1, :], w[1, :, 0:2, :].rearrange("p s n -> p (s n)")).then_inc(w_first[2], 16)
            sp.dma_start(stage[:].rearrange("p k m -> p (k m)"), w[1, :, 2, :]).then_inc(stage_ready, 16)

            def stack(cols, par, tiles, done):
                for h in range(2):
                    for tile, parts in tiles:
                        for up in range(2):
                            sp.dma_start(tile[up * D:up * D + D, par, h, cols].bitcast(F32), nat[h * D:h * D + D, parts[up], cols].bitcast(F32)).then_inc(done, 16)

            halves = [slice(0, HALF), slice(HALF, T)]

            def stack_q(cols, par):
                sp.wait_ge(q_out, 1).then_inc(q_out, -1)
                stack(cols, par, ((q_hl, (HI, LO)), (q_lh, (LO, HI))), q_stacked)

            def stack_k(cols, par):
                sp.wait_ge(k_out, 1).then_inc(k_out, -1)
                stack(cols, par, ((k_hl, (HI, LO)),), k_stacked)

            def stage_w(kind, t):
                sp.wait_ge(stage_used, 1).then_inc(stage_used, -1)
                sp.dma_start(stage[:].rearrange("p k m -> p (k m)"),
                             w[bass.ds(t, 1), :, KINDS.index(kind), :].rearrange("o p n -> (o p) n")).then_inc(stage_ready, 16)

            def store(c, at):
                sp.wait_ge(out_ready, 1).then_inc(out_ready, -1)
                sp.dma_start(y[bass.ds(at, 1), c * P:(c + 1) * P, :].rearrange("o p t -> (o p) t"), acc[:, c, :]).then_inc(stored[c], 16)

            def is_stored(c):
                sp.wait_ge(stored[c], 16).then_inc(stored[c], -16)

            def turn(i, layer, source, this, following, next_one):
                layer_next = (i + 1) // IMAGES % LAYERS
                for p in range(PAIRS):
                    after_next = layer * PAIRS + p + 2 if p < 2 else layer_next * PAIRS + p - 2
                    if p == 0:
                        sp.wait_ge(raw_used, 2 * KC).then_inc(raw_used, -2 * KC)
                        sp.dma_start(raw[:], following[bass.ds(next_one, 1)].rearrange("o (c p) t -> p (o c) t", p=P)).then_inc(raw_ready, 16)
                    stack_q(halves[0], (p + 1) % 2)
                    stage_w("o", layer * PAIRS + p)
                    if p == 0:
                        store(0, i)
                    stack_q(halves[1], (p + 1) % 2)
                    stage_w("q", after_next)
                    if p == 0:
                        for c in range(1, KC):
                            store(c, i)
                            is_stored(c - 1)
                            sp.dma_start(acc[:, c - 1, :], source[bass.ds(this, 1), (c - 1) * P:c * P, :].rearrange("o p t -> (o p) t")).then_inc(acc_ready[c - 1], 16)
                        is_stored(KC - 1)
                        sp.dma_start(acc[:, KC - 1, :], source[bass.ds(this, 1), (KC - 1) * P:C, :].rearrange("o p t -> (o p) t")).then_inc(acc_ready[KC - 1], 16)
                    for cols in halves:
                        stack_k(cols, (p + 1) % 2)
                    stage_w("k", after_next)
                    stage_w("v", after_next)

            stack_q(slice(0, T), 0)
            stack_k(slice(0, T), 0)
            with sp.Fori(0, IMAGES - 1) as i:
                turn(i, 0, x, i, x, i + 1)
            with sp.Fori(IMAGES - 1, IMAGES) as i:
                turn(i, 0, x, i, y, i - IMAGES + 2)
            with sp.Fori(IMAGES, TURNS) as i:
                turn(i, 1, y, i - IMAGES + 1, y, (i + 1) % IMAGES + 1)
            for c in range(KC):
                store(c, TURNS)
            for c in range(KC):
                is_stored(c)
            sp.wait_ge(stage_ready, 16)

        @block.tensor
        def _(pe):
            taken_by = [None, None]

            def start_small(key):
                n = bank[key]
                pe.wait_ge(small_free[n], 1).then_inc(small_free[n], -1)
                taken_by[n] = key
                return ps_m[n]

            def project_in(kind, key, half):
                if half == 0:
                    pe.wait_ge(w_ready[kind], 1).then_inc(w_ready[kind], -1)
                out = start_small(key)
                cols = slice(half * HALF, (half + 1) * HALF)
                terms = [(wl, xl, k) for k in range(KC) for wl, xl in ((HI, HI), (HI, LO), (LO, HI))]
                for n, (wl, xl, k) in enumerate(terms):
                    last = nc.tensor.matmul(out[:], wt[kind][:, wl, k, :], xs[:, xl, k, cols], start=n == 0, stop=n == len(terms) - 1)
                last.then_inc(to_act, 1)

            def scores(u, par):
                pe.wait_ge(scores_free, 1).then_inc(scores_free, -1)
                h, qb = head_of(u), u // 2
                for half in range(2):
                    cols = slice(half * HALF, (half + 1) * HALF)
                    for n, q in enumerate((q_hl, q_lh)):
                        last = nc.tensor.matmul(ps_s[u % 2][:, cols], q[:, par, h, qb * P:(qb + 1) * P], k_hl[:, par, h, cols], start=n == 0, stop=n == 1)
                last.then_inc(scores_ready, 1)

            def transposes(u):
                pe.wait_ge(probs_ready, 1).then_inc(probs_ready, -1)
                for s in range(2):
                    pe.wait_ge(t_lo, 1).then_inc(t_lo, -1)
                    for c in range(4 * s, 4 * s + 4):
                        last = nc.tensor.transpose(ps_t[:, c * P:(c + 1) * P], probs[u % 4][:, c * P:(c + 1) * P], ident[:])
                    last.then_inc(t_ready, 1)

            def attend(key, h):
                out = start_small(key)
                for c in range(NC8):
                    for part in (HI, LO):
                        last = nc.tensor.matmul(out[:, 0:256], vst[:, c, 2 * h:2 * h + 2, :].rearrange("p a d -> p (a d)"), pt[part][:, h, c, :],
                                                start=c == 0 and part == HI, stop=c == NC8 - 1 and part == LO)
                last.then_inc(to_act, 1)

            def turn_v(key, half):
                out = start_small(key)
                for c in range(4):
                    last = nc.tensor.transpose(out[:, c * P:(c + 1) * P], vt[:, (4 * half + c) * P:(4 * half + c + 1) * P], ident[:])
                last.then_inc(to_act, 1)

            def project_out(key, c):
                out = start_small(key)
                for n, (wl, o) in enumerate(((HI, o_hi), (HI, o_lo), (LO, o_hi))):
                    last = nc.tensor.matmul(out[:], wt["o"][:, wl, c, :], o[:], start=n == 0, stop=n == 2)
                last.then_inc(to_dve, 1)

            def group_mean(key):
                pe.wait_ge(moments_ready, 1).then_inc(moments_ready, -1)
                out = start_small(key)
                nc.tensor.matmul(out[:, 0:2 * KC], averager[:], moments[:].rearrange("p c s -> p (c s)"), start=True, stop=True).then_inc(to_dve, 1)

            def group_var(key):
                pe.wait_ge(moments_ready, 1).then_inc(moments_ready, -1)
                out = start_small(key)
                nc.tensor.matmul(out[:, 0:KC], averager[:], cvar[:], start=True, stop=True).then_inc(to_dve, 1)

            def read_out(key):
                if taken_by[bank[key]] == key:
                    pe.wait_ge(small_free[bank[key]], 1)

            def run(key):
                kind = key[1]
                if kind == "pv":
                    attend(key, key[2])
                elif kind == "vt":
                    turn_v(key, key[2])
                elif kind == "proj":
                    if key[2:] == (0, 0):
                        pe.wait_ge(w_ready["o"], 1).then_inc(w_ready["o"], -1)
                    if key[3] == 0:
                        pe.wait_ge(o_split, 1).then_inc(o_split, -1)
                    project_out(key, key[3])
                elif kind in "qkv":
                    project_in(kind, key, key[2])
                elif kind == "mean":
                    group_mean(key)
                elif kind == "var":
                    group_var(key)

            pe.wait_ge(const_ready, 3)
            group_mean((STATS_PAIR, "mean"))
            group_var((STATS_PAIR, "var"))
            pe.wait_ge(x_split, 2 * KC).then_inc(x_split, -2 * KC)
            for kind, half in (("q", 0), ("q", 1), ("v", 0), ("v", 1), ("k", 0), ("k", 1)):
                run((3, kind, half))
                if (kind, half) == ("v", 0):
                    read_out((3, "q", 1))
                    pe.sem_inc(q_out, 1)
            for half in range(2):
                read_out((3, "k", half))
            pe.sem_inc(k_out, 1)
            pe.wait_ge(q_stacked, Q_STACK).then_inc(q_stacked, -Q_STACK)
            pe.wait_ge(k_stacked, K_STACK).then_inc(k_stacked, -K_STACK)
            for u in range(3):
                scores(u, 0)

            with pe.Fori(0, TURNS):
                for p in range(PAIRS):
                    par = p % 2
                    for u, (between, after) in enumerate(zip(*schedule(p))):
                        transposes(u)
                        if p == 0 and ACC_OUT_SLOT <= u < ACC_OUT_SLOT + KC:
                            read_out((p, "proj", 1, u - ACC_OUT_SLOT))
                            pe.sem_inc(acc_done, 1)
                        if p == PAIRS - 1 and between in (("q", 0), ("q", 1)):
                            pe.wait_ge(x_split, KC).then_inc(x_split, -KC)
                        if between:
                            run((p, *between))
                        if u in O_OUT_SLOTS:
                            read_out((p, "pv", 1, 3 if u == O_OUT_SLOTS[0] else 1))
                            pe.sem_inc(o_out, 1)
                        if u in Q_OUT_SLOTS:
                            read_out((p, "q", Q_OUT_SLOTS.index(u)))
                            pe.sem_inc(q_out, 1)
                        if u in K_OUT_SLOTS:
                            read_out((p, "k", K_OUT_SLOTS.index(u)))
                            pe.sem_inc(k_out, 1)
                        if u + 3 == SLOTS:
                            pe.wait_ge(k_stacked, 2 * K_STACK).then_inc(k_stacked, -2 * K_STACK)
                        scores((u + 3) % SLOTS, par if u + 3 < SLOTS else 1 - par)
                        if after:
                            run((p, *after))
            pe.wait_ge(t_lo, 2).then_inc(t_lo, -2)
            run((0, "pv", 1, 3))
            read_out((0, "pv", 1, 3))
            pe.sem_inc(o_out, 1)
            for c in range(KC):
                run((0, "proj", 1, c))
            read_out((0, "proj", 1, 2))
            read_out((0, "proj", 1, 3))
            pe.sem_inc(acc_done, KC)

        @block.scalar
        def _(act):
            def exps(u):
                act.wait_ge(max_ready, 1).then_inc(max_ready, -1)
                nc.scalar.activation(probs[u % 4][:], ps_s[u % 2][:], ACT.Exp, bias=neg_max[:, u % 2:u % 2 + 1],
                                     accum_out=row_sum[:, u % 2:u % 2 + 1]).then_inc(exp_done, 1)

            def round_qk(p, name, half, bias_ap):
                act.wait_ge(to_act, 1).then_inc(to_act, -1)
                nc.scalar.activation(nat[:, HI, half * HALF:(half + 1) * HALF], ps_m[bank[(p, name, half)]][:], ACT.Identity, bias=bias_ap).then_inc(hi_out, 1)

            def round_v(p, half):
                act.wait_ge(to_act, 1).then_inc(to_act, -1)
                nc.scalar.activation(vst[:, 4 * half:4 * half + 4, 0:4:3, :], ps_m[bank[(p, "vt", half)]][:].rearrange("p (c h d) -> p c h d", c=4, h=2), ACT.Copy).then_inc(hi_out, 1)

            def finish(c, at):
                act.wait_ge(acc_done, 1).then_inc(acc_done, -1)
                nc.scalar.activation(acc[:, c, :], acc[:, c, :], ACT.Identity, bias=obias[:, bass.ds(at, 1), c:c + 1].rearrange("p o c -> p (o c)"),
                                     scale=oscale[:, bass.ds(at, 1)]).then_inc(out_ready, 1)

            def round_t(u):
                h, q = head_of(u), u // 2 % 2 * P
                for s in range(2):
                    act.wait_ge(t_ready, 1).then_inc(t_ready, -1)
                    nc.scalar.activation(pt[HI][:, h, 4 * s:4 * s + 4, q:q + P], ps_t[:, s * BANK:(s + 1) * BANK].rearrange("p (c q) -> p c q", q=P), ACT.Copy).then_inc(t_hi, 1)

            def run(p, item, bias_of):
                if item is None:
                    return
                kind, *where = item
                if kind == "pv":
                    far_half(p, *where)
                elif kind == "vt":
                    round_v(p, where[0])
                elif kind in ("q", "k"):
                    if (kind, *where) == ("k", 0):
                        act.wait_ge(q_stacked, 2 * Q_STACK).then_inc(q_stacked, -2 * Q_STACK)
                    round_qk(p, kind, where[0], bias_of("qk".index(kind)))
                elif kind == "v":
                    add_bias_v(p, where[0], bias_of(2))

            def add_bias_v(p, half, bias_ap):
                act.wait_ge(to_act, 1).then_inc(to_act, -1)
                n = bank[(p, "v", half)]
                nc.scalar.activation(vt[:, half * HALF:(half + 1) * HALF], ps_m[n][:], ACT.Identity, bias=bias_ap).then_inc(small_free[n], 1)

            def far_half(p, h, qt):
                act.wait_ge(to_act, 1).then_inc(to_act, -1)
                nc.scalar.activation(o_half[h * D:(h + 1) * D, :], ps_m[bank[(p, "pv", h, qt)]][(1 - h) * D:(2 - h) * D, 0:256], ACT.Copy).then_inc(hi_out, 1)

            def normalise(c):
                nc.scalar.activation(raw[:, c, :], raw[:, c, :], ACT.Identity, bias=coef_b[:, c:c + 1], scale=coef_a[:, c:c + 1]).then_inc(xn_ready, 1)

            def round_w(kind, source):
                nc.scalar.activation(wt[kind][:, HI], source, ACT.Copy, scale=SCALE if kind == "q" else 1.0).then_inc(wq_hi if kind == "q" else w_hi, 1)

            def round_staged(kind):
                act.wait_ge(stage_ready, 16).then_inc(stage_ready, -16)
                round_w(kind, stage[:])

            def round_o():
                act.wait_ge(o_out, 1).then_inc(o_out, -1)
                nc.scalar.activation(o_hi[:], o_sum[:], ACT.Copy).then_inc(o_hi_done, 1)

            act.wait_ge(w_first[0], 16)
            round_w("q", first_w(0, "q"))
            round_w("k", first_w(0, "k"))
            act.wait_ge(w_first[1], 16)
            round_w("v", first_w(0, "v"))
            act.wait_ge(coef_ready, 1).then_inc(coef_ready, -1)
            for c in range(KC):
                normalise(c)
            for half in range(2):
                round_qk(3, "q", half, bias[:, 0, 0:1])
            act.wait_ge(w_first[2], 16)
            round_w("q", first_w(1, "q"))
            for half in range(2):
                add_bias_v(3, half, bias[:, 0, 2:3])
            act.wait_ge(q_stacked, Q_STACK)
            for half in range(2):
                round_qk(3, "k", half, bias[:, 0, 1:2])
            round_w("k", first_w(1, "k"))
            exps(0)
            exps(1)

            with act.Fori(0, TURNS) as i:
                layer = i // IMAGES
                layer_next = (i + 1) // IMAGES % LAYERS
                layer_last = (i + TURNS - 1) // IMAGES % LAYERS
                for p in range(PAIRS):
                    pair = layer * PAIRS + p + 1 if p < 3 else layer_next * PAIRS

                    def bias_of(j):
                        return bias[:, bass.ds(pair, 1), j:j + 1].rearrange("p o j -> p (o j)")

                    after_last = None
                    for u, (between, after) in enumerate(zip(*schedule(p))):
                        if u - 1 in O_OUT_SLOTS:
                            round_o()
                        run(p, after_last, bias_of)
                        round_t(u)
                        exps((u + 2) % SLOTS)
                        run(p, between, bias_of)
                        after_last = after
                        if p == 0 and ACC_OUT_SLOT <= u < ACC_OUT_SLOT + KC:
                            finish(u - ACC_OUT_SLOT, layer_last)
                        for kind, (hi_slot, _) in SPLIT_W.items():
                            if u == hi_slot:
                                round_staged(kind)
                        if p == NORM_PAIR and NORM_SLOT <= u < NORM_SLOT + KC:
                            if u == NORM_SLOT:
                                act.wait_ge(coef_ready, 1).then_inc(coef_ready, -1)
                            normalise(u - NORM_SLOT)
            far_half(0, 1, 3)
            round_o()
            for c in range(KC):
                finish(c, LAYERS - 1)

        @block.vector
        def _(dve):
            def own(instruction):
                instruction.then_inc(dve_own, 1)
                dve.wait_ge(dve_own, 1).then_inc(dve_own, -1)

            def maxima(u):
                dve.wait_ge(scores_ready, 1).then_inc(scores_ready, -1)
                nc.vector.tensor_reduce(neg_max[:, u % 2:u % 2 + 1], ps_s[u % 2][:], AX_X, ALU.max, negate=True).then_inc(max_ready, 1)

            def inverse(u):
                dve.wait_ge(exp_done, 1).then_inc(exp_done, -1)
                dve.sem_inc(scores_free, 1)
                nc.vector.reciprocal(row_inv[:, u % 4:u % 4 + 1], row_sum[:, u % 2:u % 2 + 1]).then_inc(inv_ready, 1)

            def rest_qk(p, name, half, bias_ap):
                dve.wait_ge(hi_out, 1).then_inc(hi_out, -1)
                n = bank[(p, name, half)]
                cols = slice(half * HALF, (half + 1) * HALF)
                nc.vector.scalar_tensor_tensor(out=nat[:, LO, cols], in0=ps_m[n][:], scalar=bias_ap, in1=nat[:, HI, cols].bitcast(F32),
                                               op0=ALU.add, op1=ALU.subtract).then_inc(small_free[n], 1)

            def sum_halves(p, h, qt):
                dve.wait_ge(hi_out, 1).then_inc(hi_out, -1)
                n = bank[(p, "pv", h, qt)]
                rows = slice(h * D, (h + 1) * D)
                nc.vector.tensor_tensor(o_sum[rows, (qt % 2) * 256:(qt % 2 + 1) * 256], ps_m[n][rows, 0:256], o_half[rows, :], ALU.add).then_inc(small_free[n], 1)

            def add_projection(p, half, c):
                dve.wait_ge(to_dve, 1).then_inc(to_dve, -1)
                n = bank[(p, "proj", half, c)]
                cols = slice(half * HALF, (half + 1) * HALF)
                nc.vector.tensor_tensor(acc[:, c, cols], ps_m[n][:], acc[:, c, cols], ALU.add).then_inc(small_free[n], 1)

            def channel_stats(n):
                c, half = n // 2, n % 2
                nc.vector.bn_stats(stats[:, c, half, :], raw[:, c, half * HALF:(half + 1) * HALF]).then_inc(dve_own, 1)

            def channel_moments():
                dve.wait_ge(dve_own, 2 * KC).then_inc(dve_own, -2 * KC)
                for c in range(KC):
                    last = nc.vector.bn_aggr(moments[:, c, :], stats[:, c])
                last.then_inc(moments_ready, 1)

            def last_step():
                dve.wait_ge(dve_own, 1).then_inc(dve_own, -1)

            def group_mean():
                dve.wait_ge(to_dve, 1).then_inc(to_dve, -1)
                n = bank[(STATS_PAIR, "mean")]
                own(nc.vector.tensor_copy(gmean[:], ps_m[n][:, 0:2 * KC].rearrange("p (c s) -> p c s", s=2)[:, :, 0]))
                dve.sem_inc(small_free[n], 1)

            def deviation():
                nc.vector.tensor_tensor(cvar[:], moments[:, :, 0], gmean[:], ALU.subtract).then_inc(dve_own, 1)

            def deviation_squared():
                last_step()
                nc.vector.tensor_tensor(cvar[:], cvar[:], cvar[:], ALU.mult).then_inc(dve_own, 1)

            def channel_variance():
                last_step()
                nc.vector.tensor_tensor(cvar[:], cvar[:], moments[:, :, 1], ALU.add).then_inc(moments_ready, 1)

            def group_variance():
                dve.wait_ge(to_dve, 1).then_inc(to_dve, -1)
                n = bank[(STATS_PAIR, "var")]
                own(nc.vector.tensor_scalar(rstd[:], ps_m[n][:, 0:KC], EPS, None, ALU.add))
                dve.sem_inc(small_free[n], 1)
                dve.sem_inc(var_ready, 1)

            def coef_1(at):
                dve.wait_ge(rstd_ready, 1).then_inc(rstd_ready, -1)
                nc.vector.tensor_tensor(coef_a0[:], rstd[:], gnw[:, bass.ds(at, 1), :].rearrange("p o c -> p (o c)"), ALU.mult).then_inc(dve_own, 1)

            def coef_2(at):
                last_step()
                nc.vector.tensor_tensor(coef_b[:], gmean[:], coef_a0[:], ALU.mult).then_inc(dve_own, 1)

            def coef_3(at):
                last_step()
                nc.vector.tensor_tensor(coef_b[:], gnb[:, bass.ds(at, 1), :].rearrange("p o c -> p (o c)"), coef_b[:], ALU.subtract).then_inc(dve_own, 1)

            def coef_4(at):
                last_step()
                nc.vector.tensor_scalar(coef_b[:], coef_b[:], gate[:, bass.ds(at, 1), 0:1].rearrange("p o c -> p (o c)"), None, ALU.mult).then_inc(dve_own, 1)

            def coef_5(at):
                last_step()
                nc.vector.tensor_scalar(coef_a[:], coef_a0[:], gate[:, bass.ds(at, 1), 0:1].rearrange("p o c -> p (o c)"),
                                        gate[:, bass.ds(at, 1), 1:2].rearrange("p o c -> p (o c)"), ALU.mult, ALU.add).then_inc(coef_ready, 1)

            def round_x(half, c):
                cols = slice(half * HALF, (half + 1) * HALF)
                nc.vector.tensor_copy(xs[:, HI, c, cols], raw[:, c, cols]).then_inc(x_hi, 1)

            def rest_wq(source):
                dve.wait_ge(wq_hi, 1).then_inc(wq_hi, -1)
                nc.vector.scalar_tensor_tensor(out=wt["q"][:, LO], in0=source, scalar=SCALE, in1=wt["q"][:, HI].bitcast(F32),
                                               op0=ALU.mult, op1=ALU.subtract).then_inc(wq_lo, 1)

            def pass_wq():
                dve.wait_ge(wq_lo, 1).then_inc(wq_lo, -1)
                dve.sem_inc(w_ready["q"], 1)

            def rest_v(p, half):
                dve.wait_ge(hi_out, 1).then_inc(hi_out, -1)
                n = bank[(p, "vt", half)]
                nc.vector.tensor_tensor(vst[:, 4 * half:4 * half + 4, 1:3, :], ps_m[n][:].rearrange("p (c h d) -> p c h d", c=4, h=2),
                                        vst[:, 4 * half:4 * half + 4, 0:4:3, :].bitcast(F32), ALU.subtract).then_inc(small_free[n], 1)

            def rest_t(u):
                h, q = head_of(u), u // 2 % 2 * P
                for s in range(2):
                    dve.wait_ge(t_hi, 1).then_inc(t_hi, -1)
                    nc.vector.tensor_tensor(pt[LO][:, h, 4 * s:4 * s + 4, q:q + P], ps_t[:, s * BANK:(s + 1) * BANK].rearrange("p (c q) -> p c q", q=P),
                                            pt[HI][:, h, 4 * s:4 * s + 4, q:q + P].bitcast(F32), ALU.subtract).then_inc(t_lo, 1)

            def run(p, item, bias_of):
                if item is None:
                    return
                kind, *where = item
                if kind == "pv":
                    sum_halves(p, *where)
                elif kind == "vt":
                    rest_v(p, where[0])
                elif kind in ("q", "k"):
                    rest_qk(p, kind, where[0], bias_of("qk".index(kind)))
                elif kind == "proj":
                    half, c = where
                    if p == 0 and half == 0:
                        dve.wait_ge(acc_ready[c], 16).then_inc(acc_ready[c], -16)
                    add_projection(p, half, c)

            nc.vector.memset(vst[:].rearrange("p c a d -> p (c a d)").bitcast(F32), 0.0)
            nc.vector.memset(acc[:, 2, BANK:], 0.0)
            nc.vector.memset(acc[:, 3, :], 0.0)
            nc.vector.memset(o_sum[:], 0.0)
            nc.vector.memset(gate[:, 0, 0:1], 1.0)
            nc.vector.memset(gate[:, 0, 1:2], 0.0)
            nc.vector.memset(gate[:, 1, 0:1], 0.0)
            nc.vector.memset(gate[:, 1, 1:2], 1.0)
            nc.vector.memset(gnw[:, 1, :], 0.0)
            nc.vector.memset(gnb[:, 1, :], 0.0)
            nc.vector.memset(oscale[:, 0:1], 2.0 ** -0.5)
            own(nc.vector.memset(oscale[:, 1:2], 1.0))
            for n in range(2):
                dve.sem_inc(small_free[n], 1)
            dve.sem_inc(scores_free, 2)
            dve.sem_inc(t_lo, 2)
            for c in range(KC):
                dve.wait_ge(raw_first[c], 16)
                channel_stats(2 * c)
                channel_stats(2 * c + 1)
            channel_moments()
            group_mean()
            deviation()
            deviation_squared()
            channel_variance()
            group_variance()
            dve.wait_ge(params, 64)
            own(nc.vector.tensor_scalar(bias[:, :, 0], bias[:, :, 0], SCALE, None, ALU.mult))
            own(nc.vector.tensor_scalar(obias[:, 0, :], obias[:, 0, :], oscale[:, 0:1], None, ALU.mult))
            for step in (coef_1, coef_2, coef_3, coef_4, coef_5):
                step(0)
            rest_wq(first_w(0, "q"))
            pass_wq()
            for c in range(KC):
                dve.wait_ge(xn_ready, 1).then_inc(xn_ready, -1)
                round_x(0, c)
                own(nc.vector.tensor_copy(xs[:, HI, c, HALF:], raw[:, c, HALF:]))
                own(nc.vector.tensor_tensor(xs[:, LO, c, HALF:], raw[:, c, HALF:], xs[:, HI, c, HALF:].bitcast(F32), ALU.subtract))
                dve.sem_inc(x_split, 1)
                dve.sem_inc(raw_used, 1)
            for kind in "qk":
                for half in range(2):
                    rest_qk(3, kind, half, bias[:, 0, KINDS.index(kind):KINDS.index(kind) + 1])
                if kind == "q":
                    rest_wq(first_w(1, "q"))
                    pass_wq()
            maxima(0)
            maxima(1)
            inverse(0)
            inverse(1)

            with dve.Fori(0, TURNS) as i:
                layer = i // IMAGES
                layer_next = (i + 1) // IMAGES % LAYERS
                for p in range(PAIRS):
                    pair = layer * PAIRS + p + 1 if p < 3 else layer_next * PAIRS

                    def bias_of(j):
                        return bias[:, bass.ds(pair, 1), j:j + 1].rearrange("p o j -> p (o j)")

                    after_last = None
                    for u, (between, after) in enumerate(zip(*schedule(p))):
                        if p == STATS_PAIR and u == MEAN_SLOT + 1:
                            group_mean()
                        if p == STATS_PAIR and u == VAR_SLOT + 1:
                            group_variance()
                        maxima((u + 2) % SLOTS)
                        if u != 1:
                            run(p, after_last, bias_of)
                        rest_t(u)
                        if u == 1:
                            run(p, after_last, bias_of)
                        inverse((u + 2) % SLOTS)
                        run(p, between, bias_of)
                        after_last = after
                        if u == SPLIT_W["q"][1]:
                            rest_wq(stage[:])
                        if u == SPLIT_W["q"][1] + 1:
                            pass_wq()
                            dve.sem_inc(stage_used, 1)
                        if (p, u) in STATS_SLOTS:
                            if (p, u) == STATS_SLOTS[0]:
                                dve.wait_ge(raw_ready, 16).then_inc(raw_ready, -16)
                            channel_stats(STATS_SLOTS.index((p, u)))
                        if p == STATS_PAIR and u == MOMENTS_SLOT:
                            channel_moments()
                        if p == STATS_PAIR and MEAN_SLOT + 1 < u <= MEAN_SLOT + 4:
                            (deviation, deviation_squared, channel_variance)[u - MEAN_SLOT - 2]()
                        if p == NORM_PAIR and 0 < u < NORM_SLOT:
                            (coef_1, coef_2, coef_3, coef_4, coef_5)[u - 1](layer_next)
                        for *at, half, c in X_SLOTS:
                            if at == [p, u]:
                                if half == 0:
                                    dve.wait_ge(xn_ready, 1).then_inc(xn_ready, -1)
                                round_x(half, c)
            sum_halves(0, 1, 3)
            for c in range(KC):
                add_projection(0, 1, c)

        @block.gpsimd
        def _(pool):
            def own(instruction):
                instruction.then_inc(pool_own, 1)
                pool.wait_ge(pool_own, 1).then_inc(pool_own, -1)

            def scale_probs(u):
                pool.wait_ge(inv_ready, 1).then_inc(inv_ready, -1)
                nc.gpsimd.tensor_tensor(probs[u % 4][:], probs[u % 4][:], row_inv[:, u % 4:u % 4 + 1].to_broadcast([P, T]), ALU.mult).then_inc(probs_ready, 1)

            def rest_o():
                pool.wait_ge(o_hi_done, 1).then_inc(o_hi_done, -1)
                nc.gpsimd.tensor_tensor(o_lo[:], o_sum[:], o_hi[:].bitcast(F32), ALU.subtract).then_inc(o_split, 1)

            def rest_x(half, c):
                pool.wait_ge(x_hi, 1).then_inc(x_hi, -1)
                cols = slice(half * HALF, (half + 1) * HALF)
                own(nc.gpsimd.tensor_tensor(xs[:, LO, c, cols], raw[:, c, cols], xs[:, HI, c, cols].bitcast(F32), ALU.subtract))
                pool.sem_inc(x_split, 1)
                pool.sem_inc(raw_used, 1)

            def rest_w(kind, source):
                pool.wait_ge(w_hi, 1).then_inc(w_hi, -1)
                own(nc.gpsimd.tensor_tensor(wt[kind][:, LO], source, wt[kind][:, HI].bitcast(F32), ALU.subtract))
                pool.sem_inc(w_ready[kind], 1)

            def inverse_root():
                pool.wait_ge(var_ready, 1).then_inc(var_ready, -1)
                nc.gpsimd.tensor_tensor(rstd[:], rstd[:], power[:], ALU.pow).then_inc(rstd_ready, 1)

            own(nc.gpsimd.memset(ident[:], 0.0))
            nc.gpsimd.affine_select(out=ident[:], in_=ident[:], compare_op=ALU.not_equal, fill=1.0, base=0,
                                    pattern=[[-1, P]], channel_multiplier=1).then_inc(const_ready, 1)
            per_group = C // GROUPS
            own(nc.gpsimd.memset(averager[:], 1.0 / per_group))
            by_group = averager[:].rearrange("p (g m) -> p g m", m=per_group)
            own(nc.gpsimd.affine_select(out=by_group, in_=by_group, compare_op=ALU.is_ge, fill=0.0, base=0,
                                        pattern=[[-per_group, P // per_group], [0, per_group]], channel_multiplier=1))
            nc.gpsimd.affine_select(out=by_group, in_=by_group, compare_op=ALU.is_ge, fill=0.0, base=per_group - 1,
                                    pattern=[[per_group, P // per_group], [0, per_group]], channel_multiplier=-1).then_inc(const_ready, 1)
            nc.gpsimd.memset(power[:], -0.5)
            nc.gpsimd.memset(wt["o"][:].rearrange("p a k m -> p (a k m)").bitcast(F32), 0.0)
            nc.gpsimd.memset(pt[HI][:, 1].rearrange("p c q -> p (c q)").bitcast(F32), 0.0)
            own(nc.gpsimd.memset(pt[LO][:, 1].rearrange("p c q -> p (c q)").bitcast(F32), 0.0))
            pool.sem_inc(const_ready, 1)
            for kind in "kv":
                rest_w(kind, first_w(0, kind))
            inverse_root()
            for c in range(KC):
                rest_x(0, c)
            rest_w("k", first_w(1, "k"))
            scale_probs(0)
            scale_probs(1)
            with pool.Fori(0, TURNS):
                for p in range(PAIRS):
                    for u in range(SLOTS):
                        if u - 1 in O_OUT_SLOTS:
                            rest_o()
                        for kind in "kvo":
                            if u == SPLIT_W[kind][1]:
                                rest_w(kind, stage[:])
                                pool.sem_inc(stage_used, 1)
                        for n in range(len(X_SLOTS)):
                            x_pair, x_slot, half, c = X_SLOTS[n]
                            if (p, u) == (x_pair + (x_slot + 1) // SLOTS, (x_slot + 1) % SLOTS):
                                rest_x(half, c)
                        scale_probs((u + 2) % SLOTS)
                        if p == NORM_PAIR and u == 0:
                            inverse_root()
            rest_o()


def kernel(x, L0_conv_gn_w, L0_conv_gn_b, L0_conv_qkv_w, L0_conv_qkv_b, L0_conv_proj_w, L0_conv_proj_b,
           L1_conv_w_qkv, L1_conv_b_qkv, L1_conv_w_proj, L1_conv_b_proj):
    import numpy as np
    import concourse.bacc as bacc
    from concourse.bass_utils import run_bass_kernel_spmd

    B, C, H, W = x.shape
    pairs, d = HEADS // 2, C // HEADS

    def lay_in(w_in, w_out):
        q = np.asarray(w_in).reshape(C // P, P, pairs, 2, 3, d).transpose(2, 1, 4, 0, 3, 5).reshape(pairs, P, 3, C)
        o = np.asarray(w_out).reshape(pairs, P, 1, C)
        return np.concatenate([q, o], 2)

    def lay_bias(v):
        return np.asarray(v).reshape(pairs, 2, 3, d).transpose(0, 1, 3, 2).reshape(pairs, P, 3)

    def lay_channels(v):
        return np.asarray(v).reshape(C // P, P).T

    arrays = {
        "x": np.asarray(x).reshape(B, C, H * W),
        "w": np.concatenate([lay_in(np.asarray(L0_conv_qkv_w).T, np.asarray(L0_conv_proj_w).T), lay_in(L1_conv_w_qkv, L1_conv_w_proj)]),
        "b": np.concatenate([lay_bias(L0_conv_qkv_b), lay_bias(L1_conv_b_qkv)]),
        "gn": np.stack([lay_channels(L0_conv_gn_w), lay_channels(L0_conv_gn_b)]),
        "pb": np.stack([lay_channels(L0_conv_proj_b), lay_channels(L1_conv_b_proj)]),
    }
    arrays = {k: np.ascontiguousarray(a) for k, a in arrays.items()}
    nc = bacc.Bacc("TRN2", target_bir_lowering=False, num_devices=1)
    aps = [nc.dram_tensor(n, a.shape, mybir.dt.from_np(a.dtype), kind="ExternalInput").ap() for n, a in arrays.items()]
    y = nc.dram_tensor("y", (2 * B + 1, C, H * W), F32, kind="ExternalOutput").ap()
    build(nc, *aps, y)
    r = run_bass_kernel_spmd(nc, [arrays], core_ids=[0])
    return r.results[0]["y"][B + 1:].reshape(B, C, H, W)
```
